# Optimizing a Trainium2 kernel written in Bass

```python
import numpy as np
import jax
import jax.numpy as jnp

def _softmax(x, axis=-1):
    return jax.nn.softmax(x, axis=axis)

def _gelu(x):
    return jax.nn.gelu(x, approximate=True)

def _silu(x):
    return jax.nn.silu(x)

def _sigmoid(x):
    return jax.nn.sigmoid(x)

def _layernorm(x, axis=-1, eps=1e-05):
    m = jnp.mean(x, axis=axis, keepdims=True)
    v = jnp.var(x, axis=axis, keepdims=True)
    return (x - m) / jnp.sqrt(v + eps)

def _scatter_add(tgt, idx, src, axis=0):
    return tgt.at[idx].add(src)

def _segment_sum(src, seg, n):
    return jax.ops.segment_sum(src, seg, n)
kernel_name = 'mk_dlrm_tower_d1_rec_r8_e83bab'

def setup_inputs(seed: int=0):
    np.random.seed(seed)
    _w = jnp.asarray

    def _rec_inputs():
        import jax
        import jax.numpy as jnp
        _tk = jax.random.key(seed)
        dense_ctx = jax.random.normal(jax.random.fold_in(_tk, 190), (512, 16), jnp.float32)
        ids = jnp.stack([jax.random.randint(jax.random.fold_in(_tk, 200 + f), (512,), 0, v, jnp.int32) for f, v in enumerate([1250, 125000, 1000, 1000, 1000, 125000, 1250, 12500, 125000, 1250, 1250, 1000, 1000, 1000, 1000, 12500, 1250, 125000, 12500, 12500, 12500, 12500, 1000, 125000, 125000, 12500, 12500, 1000, 1250, 1250, 12500, 1250, 1000, 1250, 1000, 125000, 1000, 125000, 1000])], axis=1)
        tbl_0 = 0.05 * jax.random.normal(jax.random.fold_in(_tk, 500 + 0), (1250, 16), jnp.float32)
        tbl_1 = 0.05 * jax.random.normal(jax.random.fold_in(_tk, 500 + 1), (125000, 16), jnp.float32)
        tbl_2 = 0.05 * jax.random.normal(jax.random.fold_in(_tk, 500 + 2), (1000, 16), jnp.float32)
        tbl_3 = 0.05 * jax.random.normal(jax.random.fold_in(_tk, 500 + 3), (1000, 16), jnp.float32)
        tbl_4 = 0.05 * jax.random.normal(jax.random.fold_in(_tk, 500 + 4), (1000, 16), jnp.float32)
        tbl_5 = 0.05 * jax.random.normal(jax.random.fold_in(_tk, 500 + 5), (125000, 16), jnp.float32)
        tbl_6 = 0.05 * jax.random.normal(jax.random.fold_in(_tk, 500 + 6), (1250, 16), jnp.float32)
        tbl_7 = 0.05 * jax.random.normal(jax.random.fold_in(_tk, 500 + 7), (12500, 16), jnp.float32)
        tbl_8 = 0.05 * jax.random.normal(jax.random.fold_in(_tk, 500 + 8), (125000, 16), jnp.float32)
        tbl_9 = 0.05 * jax.random.normal(jax.random.fold_in(_tk, 500 + 9), (1250, 16), jnp.float32)
        tbl_10 = 0.05 * jax.random.normal(jax.random.fold_in(_tk, 500 + 10), (1250, 16), jnp.float32)
        tbl_11 = 0.05 * jax.random.normal(jax.random.fold_in(_tk, 500 + 11), (1000, 16), jnp.float32)
        tbl_12 = 0.05 * jax.random.normal(jax.random.fold_in(_tk, 500 + 12), (1000, 16), jnp.float32)
        tbl_13 = 0.05 * jax.random.normal(jax.random.fold_in(_tk, 500 + 13), (1000, 16), jnp.float32)
        tbl_14 = 0.05 * jax.random.normal(jax.random.fold_in(_tk, 500 + 14), (1000, 16), jnp.float32)
        tbl_15 = 0.05 * jax.random.normal(jax.random.fold_in(_tk, 500 + 15), (12500, 16), jnp.float32)
        tbl_16 = 0.05 * jax.random.normal(jax.random.fold_in(_tk, 500 + 16), (1250, 16), jnp.float32)
        tbl_17 = 0.05 * jax.random.normal(jax.random.fold_in(_tk, 500 + 17), (125000, 16), jnp.float32)
        tbl_18 = 0.05 * jax.random.normal(jax.random.fold_in(_tk, 500 + 18), (12500, 16), jnp.float32)
        tbl_19 = 0.05 * jax.random.normal(jax.random.fold_in(_tk, 500 + 19), (12500, 16), jnp.float32)
        tbl_20 = 0.05 * jax.random.normal(jax.random.fold_in(_tk, 500 + 20), (12500, 16), jnp.float32)
        tbl_21 = 0.05 * jax.random.normal(jax.random.fold_in(_tk, 500 + 21), (12500, 16), jnp.float32)
        tbl_22 = 0.05 * jax.random.normal(jax.random.fold_in(_tk, 500 + 22), (1000, 16), jnp.float32)
        tbl_23 = 0.05 * jax.random.normal(jax.random.fold_in(_tk, 500 + 23), (125000, 16), jnp.float32)
        tbl_24 = 0.05 * jax.random.normal(jax.random.fold_in(_tk, 500 + 24), (125000, 16), jnp.float32)
        tbl_25 = 0.05 * jax.random.normal(jax.random.fold_in(_tk, 500 + 25), (12500, 16), jnp.float32)
        tbl_26 = 0.05 * jax.random.normal(jax.random.fold_in(_tk, 500 + 26), (12500, 16), jnp.float32)
        tbl_27 = 0.05 * jax.random.normal(jax.random.fold_in(_tk, 500 + 27), (1000, 16), jnp.float32)
        tbl_28 = 0.05 * jax.random.normal(jax.random.fold_in(_tk, 500 + 28), (1250, 16), jnp.float32)
        tbl_29 = 0.05 * jax.random.normal(jax.random.fold_in(_tk, 500 + 29), (1250, 16), jnp.float32)
        tbl_30 = 0.05 * jax.random.normal(jax.random.fold_in(_tk, 500 + 30), (12500, 16), jnp.float32)
        tbl_31 = 0.05 * jax.random.normal(jax.random.fold_in(_tk, 500 + 31), (1250, 16), jnp.float32)
        tbl_32 = 0.05 * jax.random.normal(jax.random.fold_in(_tk, 500 + 32), (1000, 16), jnp.float32)
        tbl_33 = 0.05 * jax.random.normal(jax.random.fold_in(_tk, 500 + 33), (1250, 16), jnp.float32)
        tbl_34 = 0.05 * jax.random.normal(jax.random.fold_in(_tk, 500 + 34), (1000, 16), jnp.float32)
        tbl_35 = 0.05 * jax.random.normal(jax.random.fold_in(_tk, 500 + 35), (125000, 16), jnp.float32)
        tbl_36 = 0.05 * jax.random.normal(jax.random.fold_in(_tk, 500 + 36), (1000, 16), jnp.float32)
        tbl_37 = 0.05 * jax.random.normal(jax.random.fold_in(_tk, 500 + 37), (125000, 16), jnp.float32)
        tbl_38 = 0.05 * jax.random.normal(jax.random.fold_in(_tk, 500 + 38), (1000, 16), jnp.float32)
        _rk = jax.random.fold_in(_tk, 7)
        W_top1 = 0.05 * jax.random.normal(jax.random.fold_in(_tk, 801), (400, 512), jnp.float32)
        W_top2 = 0.0441942 * jax.random.normal(jax.random.fold_in(_tk, 802), (512, 256), jnp.float32)
        W_top3 = 0.0625 * jax.random.normal(jax.random.fold_in(_tk, 803), (256, 1), jnp.float32)
        b_top1 = jnp.zeros((512,), jnp.float32)
        b_top2 = jnp.zeros((256,), jnp.float32)
        return (dense_ctx, ids, tbl_0, tbl_1, tbl_2, tbl_3, tbl_4, tbl_5, tbl_6, tbl_7, tbl_8, tbl_9, tbl_10, tbl_11, tbl_12, tbl_13, tbl_14, tbl_15, tbl_16, tbl_17, tbl_18, tbl_19, tbl_20, tbl_21, tbl_22, tbl_23, tbl_24, tbl_25, tbl_26, tbl_27, tbl_28, tbl_29, tbl_30, tbl_31, tbl_32, tbl_33, tbl_34, tbl_35, tbl_36, tbl_37, tbl_38, W_top1, b_top1, W_top2, b_top2, W_top3)
    dense_ctx, ids, tbl_0, tbl_1, tbl_2, tbl_3, tbl_4, tbl_5, tbl_6, tbl_7, tbl_8, tbl_9, tbl_10, tbl_11, tbl_12, tbl_13, tbl_14, tbl_15, tbl_16, tbl_17, tbl_18, tbl_19, tbl_20, tbl_21, tbl_22, tbl_23, tbl_24, tbl_25, tbl_26, tbl_27, tbl_28, tbl_29, tbl_30, tbl_31, tbl_32, tbl_33, tbl_34, tbl_35, tbl_36, tbl_37, tbl_38, W_top1, b_top1, W_top2, b_top2, W_top3 = _rec_inputs()

    def _L0_rec_setup():
        import jax, jax.numpy as jnp
        import numpy as np
        B, F0, D = (256, 39, 16)
        CROSS = [128, 128, 128]
        key = jax.random.key(seed)
        k0, k1, k2, k3 = jax.random.split(key, 4)
        inputs = jax.random.normal(k0, (B, F0, D), dtype=jnp.float32)
        f0 = jax.random.normal(k1, (F0 * F0, CROSS[0]), dtype=jnp.float32) * 0.05
        f1 = jax.random.normal(k2, (CROSS[0] * F0, CROSS[1]), dtype=jnp.float32) * 0.05
        f2 = jax.random.normal(k3, (CROSS[1] * F0, CROSS[2]), dtype=jnp.float32) * 0.05
        return {'inputs': inputs, 'f0': f0, 'f1': f1, 'f2': f2}
    _L0_rec_all = _L0_rec_setup()
    _L0_rec_in = {k: v for k, v in _L0_rec_all.items() if k in ('f0', 'f1', 'f2')}
    del _L0_rec_all
    return {'dense_ctx': dense_ctx, 'ids': ids, 'tbl_0': tbl_0, 'tbl_1': tbl_1, 'tbl_2': tbl_2, 'tbl_3': tbl_3, 'tbl_4': tbl_4, 'tbl_5': tbl_5, 'tbl_6': tbl_6, 'tbl_7': tbl_7, 'tbl_8': tbl_8, 'tbl_9': tbl_9, 'tbl_10': tbl_10, 'tbl_11': tbl_11, 'tbl_12': tbl_12, 'tbl_13': tbl_13, 'tbl_14': tbl_14, 'tbl_15': tbl_15, 'tbl_16': tbl_16, 'tbl_17': tbl_17, 'tbl_18': tbl_18, 'tbl_19': tbl_19, 'tbl_20': tbl_20, 'tbl_21': tbl_21, 'tbl_22': tbl_22, 'tbl_23': tbl_23, 'tbl_24': tbl_24, 'tbl_25': tbl_25, 'tbl_26': tbl_26, 'tbl_27': tbl_27, 'tbl_28': tbl_28, 'tbl_29': tbl_29, 'tbl_30': tbl_30, 'tbl_31': tbl_31, 'tbl_32': tbl_32, 'tbl_33': tbl_33, 'tbl_34': tbl_34, 'tbl_35': tbl_35, 'tbl_36': tbl_36, 'tbl_37': tbl_37, 'tbl_38': tbl_38, 'W_top1': W_top1, 'b_top1': b_top1, 'W_top2': W_top2, 'b_top2': b_top2, 'W_top3': W_top3, 'L0_rec_f0': _L0_rec_in['f0'], 'L0_rec_f1': _L0_rec_in['f1'], 'L0_rec_f2': _L0_rec_in['f2']}

def reference(dense_ctx, ids, tbl_0, tbl_1, tbl_2, tbl_3, tbl_4, tbl_5, tbl_6, tbl_7, tbl_8, tbl_9, tbl_10, tbl_11, tbl_12, tbl_13, tbl_14, tbl_15, tbl_16, tbl_17, tbl_18, tbl_19, tbl_20, tbl_21, tbl_22, tbl_23, tbl_24, tbl_25, tbl_26, tbl_27, tbl_28, tbl_29, tbl_30, tbl_31, tbl_32, tbl_33, tbl_34, tbl_35, tbl_36, tbl_37, tbl_38, W_top1, b_top1, W_top2, b_top2, W_top3, L0_rec_f0, L0_rec_f1, L0_rec_f2):
    import jax
    import jax.numpy as jnp

    def _L0_rec_ref(inputs, f0, f1, f2):
        import jax, jax.numpy as jnp
        import numpy as np
        B, F0, D = (256, 39, 16)
        CROSS = [128, 128, 128]
        filters = [f0, f1, f2]
        x0 = inputs
        xk = inputs
        outs = []
        for W in filters:
            b, f, d = x0.shape
            g = xk.shape[1]
            z = jnp.einsum('bfd,bgd->bfgd', x0, xk).reshape(b, f * g, d)
            cur = jnp.einsum('bpd,pm->bmd', z, W)
            outs.append(cur)
            xk = cur
        result = jnp.concatenate(outs, axis=1)
        return jnp.sum(result, axis=-1)
    e = jnp.stack([tbl_0[ids[:, 0]], tbl_1[ids[:, 1]], tbl_2[ids[:, 2]], tbl_3[ids[:, 3]], tbl_4[ids[:, 4]], tbl_5[ids[:, 5]], tbl_6[ids[:, 6]], tbl_7[ids[:, 7]], tbl_8[ids[:, 8]], tbl_9[ids[:, 9]], tbl_10[ids[:, 10]], tbl_11[ids[:, 11]], tbl_12[ids[:, 12]], tbl_13[ids[:, 13]], tbl_14[ids[:, 14]], tbl_15[ids[:, 15]], tbl_16[ids[:, 16]], tbl_17[ids[:, 17]], tbl_18[ids[:, 18]], tbl_19[ids[:, 19]], tbl_20[ids[:, 20]], tbl_21[ids[:, 21]], tbl_22[ids[:, 22]], tbl_23[ids[:, 23]], tbl_24[ids[:, 24]], tbl_25[ids[:, 25]], tbl_26[ids[:, 26]], tbl_27[ids[:, 27]], tbl_28[ids[:, 28]], tbl_29[ids[:, 29]], tbl_30[ids[:, 30]], tbl_31[ids[:, 31]], tbl_32[ids[:, 32]], tbl_33[ids[:, 33]], tbl_34[ids[:, 34]], tbl_35[ids[:, 35]], tbl_36[ids[:, 36]], tbl_37[ids[:, 37]], tbl_38[ids[:, 38]]], axis=1)
    z = _L0_rec_ref(e, L0_rec_f0, L0_rec_f1, L0_rec_f2)
    z = z.reshape(z.shape[0], -1)
    h = jnp.concatenate([z, dense_ctx], axis=1)
    h = jnp.maximum(h @ W_top1 + b_top1, 0.0)
    h = jnp.maximum(h @ W_top2 + b_top2, 0.0)
    y = h @ W_top3
    return y

_drawn_inputs = setup_inputs


def setup_inputs(seed=0):
    import zlib

    import numpy as np

    out = dict(_drawn_inputs(seed))
    spreads = {'b_top1': (0.0, 0.605), 'b_top2': (0.0, 0.28)}
    factors = {'tbl_0': 4.428,
     'tbl_1': 4.865,
     'tbl_2': 4.733,
     'tbl_3': 5.015,
     'tbl_4': 4.989,
     'tbl_5': 5.146,
     'tbl_6': 4.784,
     'tbl_7': 4.786,
     'tbl_8': 4.974,
     'tbl_9': 4.626,
     'tbl_10': 4.823,
     'tbl_11': 4.825,
     'tbl_12': 4.523,
     'tbl_13': 4.582,
     'tbl_14': 4.878,
     'tbl_15': 5.108,
     'tbl_16': 5.24,
     'tbl_17': 4.919,
     'tbl_18': 5.054,
     'tbl_19': 5.012,
     'tbl_20': 4.972,
     'tbl_21': 4.787,
     'tbl_22': 4.655,
     'tbl_23': 4.843,
     'tbl_24': 4.781,
     'tbl_25': 4.454,
     'tbl_26': 4.966,
     'tbl_27': 5.365,
     'tbl_28': 4.726,
     'tbl_29': 4.628,
     'tbl_30': 4.945,
     'tbl_31': 4.504,
     'tbl_32': 5.038,
     'tbl_33': 4.982,
     'tbl_34': 4.643,
     'tbl_35': 4.893,
     'tbl_36': 4.787,
     'tbl_37': 5.076,
     'tbl_38': 5.125,
     'L0_rec_f1': 4.87,
     'L0_rec_f2': 8.0}
    for name, (base, spread) in spreads.items():
        noise = np.random.default_rng([zlib.crc32(name.encode()), seed]).standard_normal(out[name].shape)
        drawn = base * np.exp(spread * noise) if base else spread * noise
        out[name] = jnp.asarray(drawn.astype(out[name].dtype))
    for name, factor in factors.items():
        out[name] = (out[name] * factor).astype(out[name].dtype)
    return out
```

```python
from contextlib import ExitStack

import numpy as np

import concourse.bass as bass
from concourse import mybir
from concourse.alu_op_type import AluOpType as ALU

F32 = mybir.dt.float32
F32R = mybir.dt.float32r
I32 = mybir.dt.int32
ACT = mybir.ActivationFunctionType
AX_X = mybir.AxisListType.X

FIELDS = 39
EMB = 16
BATCH = 512
MAPS = 128
P = 128

SAMPLES = P // EMB
TILES = 4
CHUNKS = 4
GROUPS = BATCH // P
GROUP_TILES = TILES * CHUNKS
CHUNK = TILES * P
CHUNK_SAMPLES = TILES * SAMPLES

SHIFTS = (FIELDS + 1) // 2
SHIFT0 = FIELDS - SHIFTS + 1
PAIRS = SHIFTS * FIELDS
CROSS = PAIRS - FIELDS
PAIR_BLOCKS = -(-PAIRS // P)
PAIR_REST = PAIRS - (PAIR_BLOCKS - 1) * P

BANK_FIELDS = 4
BANKS = -(-FIELDS // BANK_FIELDS)
RING = 4
ACT_BANKS = (0, 2, 3, 5, 6, 8, 9)
DVE_BANKS = (1, 4, 7)
assert sorted(ACT_BANKS + DVE_BANKS) == list(range(BANKS))


def bank_fields(j):
    return range(BANK_FIELDS * j, min(BANK_FIELDS * (j + 1), FIELDS))


ACT_SLOT = {f: n for n, f in enumerate(f for j in ACT_BANKS for f in bank_fields(j))}
DVE_ORDER = [f for j in DVE_BANKS for f in bank_fields(j)]
SLOTS = len(ACT_SLOT) + 2

POS_TRANSPOSE = [(2 + 8 * i, 3 + 8 * i) for i in range(TILES)]
POS_CROSS1 = {31: (0, 1), 32: (2, 3), 33: (4, 5), 34: (6,)}
POS_FIELD_T = (18, 20, 22, 24)
POS_TILE_T = 27
POS_POOLED = 9
FIRST = 3

MLP1 = 512
MLP2 = 256
DENSE = 16
K_MLP1 = 3


def at(group, per_group, const):
    return group * per_group + const


def cin_program(nc, ids, tables, dense_t, w0_a, w0_b, w1, w2, wt1, bt1, wt2, bt2, wt3, out):
    with ExitStack() as ctx:
        def sb(name, shape, dt=F32):
            return ctx.enter_context(nc.sbuf_tensor(name, shape, dt))

        def sem(name):
            return ctx.enter_context(nc.semaphore(name))

        prod = ctx.enter_context(nc.psum_tensor("prod", [P, RING, 512], F32))
        pair_t = ctx.enter_context(nc.psum_tensor("pair_t", [P, 2, 512], F32))
        mid = ctx.enter_context(nc.psum_tensor("mid", [P, 512], F32))
        pool_ps = ctx.enter_context(nc.psum_tensor("pool_ps", [P, 512], F32))

        ids_sb = sb("ids_sb", [P, FIELDS], I32)
        rows = sb("rows", [P, FIELDS, EMB])
        x_field = sb("x_field", [FIELDS, P * EMB])
        x_col = sb("x_col", [P, CHUNKS, TILES, 2 * FIELDS])
        pairs = sb("pairs", [P, 2, PAIR_BLOCKS * P])
        pair_h = sb("pair_h", [P, PAIR_BLOCKS, CHUNK], F32R)
        pair_l = sb("pair_l", [P, PAIR_BLOCKS, CHUNK], F32R)
        w0_h = sb("w0_h", [P, PAIR_BLOCKS, MAPS], F32R)
        w0_l = sb("w0_l", [P, PAIR_BLOCKS, MAPS], F32R)
        w1_h = sb("w1_h", [P, FIELDS * MAPS], F32R)
        w1_l = sb("w1_l", [P, FIELDS * MAPS], F32R)
        w2_sb = sb("w2_sb", [P, FIELDS * MAPS])
        c1_h = sb("c1_h", [P, 2, CHUNK], F32R)
        c1_l = sb("c1_l", [P, 2, CHUNK], F32R)
        terms = sb("terms", [P, 2, SLOTS, MAPS])
        c2 = sb("c2", [P, 2, MAPS])
        x_diag = sb("x_diag", [P, TILES, SAMPLES, FIELDS + 1])
        pooled = sb("pooled", [P, FIELDS + 1, P])
        out1 = sb("out1", [P, P])
        out1_done = sb("out1_done", [P, P])
        out3 = sb("out3", [P, P])
        dense_sb = sb("dense_sb", [DENSE, BATCH])
        wt1_sb = sb("wt1_sb", [P, K_MLP1, MLP1])
        wt1_d = sb("wt1_d", [DENSE, MLP1])
        wt2_sb = sb("wt2_sb", [P, MLP1 // P, MLP2])
        wt3_sb = sb("wt3_sb", [P, MLP2 // P])
        bt1_sb = sb("bt1_sb", [P, MLP1 // P])
        bt2_sb = sb("bt2_sb", [P, MLP2 // P])
        h1 = sb("h1", [P, MLP1 // P, P])
        h2 = sb("h2", [P, MLP2 // P, P])
        y_sb = sb("y_sb", [1, P])
        ident = sb("ident", [P, P])
        own = sb("own", [P, SAMPLES])
        warm = sb("warm", [P, 1])

        w1_raw = pooled[:, :, :].rearrange("p f b -> p (f b)")[:, 0:FIELDS * MAPS]
        w0_a_raw = terms[:, 0, 0:PAIR_BLOCKS, :]
        w0_b_raw = terms[:, 0, PAIR_BLOCKS:2 * PAIR_BLOCKS, :]
        w0_sum = terms[:, 0, 2 * PAIR_BLOCKS:3 * PAIR_BLOCKS, :]

        ids_loaded = sem("ids_loaded")
        w0_loaded = sem("w0_loaded")
        w1_loaded = sem("w1_loaded")
        w2_loaded = sem("w2_loaded")
        tower_loaded = sem("tower_loaded")
        rows_loaded = sem("rows_loaded")
        consts_step = sem("consts_step")
        consts_ready = sem("consts_ready")
        w0_zeroed = sem("w0_zeroed")
        w0_summed = sem("w0_summed")
        w0_high = sem("w0_high")
        w0_ready = sem("w0_ready")
        w1_high = sem("w1_high")
        w1_ready = sem("w1_ready")
        field_t_ready = sem("field_t_ready")
        field_t_copied = sem("field_t_copied")
        tile_t_ready = sem("tile_t_ready")
        x_col_ready = sem("x_col_ready")
        pairs_ready = sem("pairs_ready")
        pair_t_ready = sem("pair_t_ready")
        pair_high = sem("pair_high")
        pair_low = sem("pair_low")
        cross1_ready = sem("cross1_ready")
        c1_high = sem("c1_high")
        c1_low = sem("c1_low")
        out1_saved = sem("out1_saved")
        out1_ready = sem("out1_ready")
        prod_ready = sem("prod_ready")
        act_bank_done = sem("act_bank_done")
        dve_unit_done = sem("dve_unit_done")
        c2_ready = sem("c2_ready")
        x_diag_ready = sem("x_diag_ready")
        pool_ready = sem("pool_ready")
        pooled_saved = sem("pooled_saved")
        cross3_ready = sem("cross3_ready")
        out3_ready = sem("out3_ready")
        h1_ready = sem("h1_ready")
        h1_saved = sem("h1_saved")
        h2_ready = sem("h2_ready")
        h2_saved = sem("h2_saved")
        y_ready = sem("y_ready")
        y_saved = sem("y_saved")
        y_stored = sem("y_stored")
        y_free = sem("y_free")

        def act_count(group, t, n):
            return at(group, len(ACT_BANKS) * GROUP_TILES, len(ACT_BANKS) * t + n)

        def dve_count(group, t, n):
            return at(group, len(DVE_ORDER) * GROUP_TILES, len(DVE_ORDER) * t + n)

        def tile_count(group, t, per_tile=1):
            return at(group, per_tile * GROUP_TILES, per_tile * t)

        def chunk_count(group, c, per_chunk=1):
            return at(group, per_chunk * CHUNKS, per_chunk * c)

        def run(step, eng, before):
            before()
            for t in range(FIRST):
                step(0, t)
            with eng.Fori(0, GROUPS - 1) as group:
                for t in range(FIRST, FIRST + GROUP_TILES):
                    step(group, t)
            for t in range(FIRST, GROUP_TILES):
                step(GROUPS - 1, t)

        def is_last(group):
            return isinstance(group, int) and group == GROUPS - 1

        def is_start(group, t):
            return isinstance(group, int) and group == 0 and t == 0

        block = ctx.enter_context(nc.Block())

        @block.sync
        def _(sp):
            sp.dma_start(ids_sb[:, :], ids[0:P, :]).then_inc(ids_loaded, 16)
            full = (PAIR_BLOCKS - 1) * P
            sp.dma_start(w0_a_raw[:, 0:PAIR_BLOCKS - 1, :],
                         w0_a[0:full, :].rearrange("(k p) m -> p k m", p=P)).then_inc(w0_loaded, 16)
            sp.dma_start(w0_a_raw[0:PAIR_REST, PAIR_BLOCKS - 1, :], w0_a[full:PAIRS, :]).then_inc(w0_loaded, 16)
            whole = CROSS // P
            sp.dma_start(w0_b_raw[:, 0:whole, :],
                         w0_b[0:whole * P, :].rearrange("(k p) m -> p k m", p=P)).then_inc(w0_loaded, 16)
            sp.wait_ge(w0_zeroed, 1)
            sp.dma_start(w0_b_raw[0:CROSS - whole * P, whole, :], w0_b[whole * P:CROSS, :]).then_inc(w0_loaded, 16)
            sp.dma_start(w1_raw.rearrange("g (f m) -> g f m", m=MAPS),
                         w1.rearrange("(f g) m -> g f m", g=MAPS)).then_inc(w1_loaded, 16)
            sp.dma_start(w2_sb[:, :].rearrange("g (f m) -> g f m", m=MAPS),
                         w2.rearrange("(f g) m -> g f m", g=MAPS)).then_inc(w2_loaded, 16)
            sp.dma_start(wt1_sb[:, :, :], wt1[0:K_MLP1 * P, :].rearrange("(k p) m -> p k m", p=P)).then_inc(tower_loaded, 16)
            sp.dma_start(wt1_d[:, :], wt1[K_MLP1 * P:, :]).then_inc(tower_loaded, 16)
            sp.dma_start(wt2_sb[:, :, :], wt2.rearrange("(k p) m -> p k m", p=P)).then_inc(tower_loaded, 16)
            sp.dma_start(wt3_sb[:, :], wt3).then_inc(tower_loaded, 16)
            sp.dma_start(bt1_sb[:, :], bt1).then_inc(tower_loaded, 16)
            sp.dma_start(bt2_sb[:, :], bt2).then_inc(tower_loaded, 16)
            sp.dma_start(dense_sb[:, :], dense_t).then_inc(tower_loaded, 16)
            with sp.Fori(0, GROUPS - 1) as group:
                sp.wait_ge(rows_loaded, at(group, 16 * FIELDS, 16 * FIELDS))
                sp.dma_start(ids_sb[:, :], ids[bass.ds(group * P + P, P), :]).then_inc(ids_loaded, 16)
                sp.wait_ge(y_stored, at(group, 16, 16))
                sp.sem_inc(y_free, 1)
            sp.wait_ge(y_stored, 16 * GROUPS)

        @block.gpsimd
        def _(pool):
            def gather(fields):
                for f in fields:
                    nc.gpsimd.indirect_dma_start(
                        rows[:, f, :], None, tables[f],
                        bass.IndirectOffsetOnAxis(ap=ids_sb[:, f:f + 1], axis=0)).then_inc(rows_loaded, 16)

            def pair_products(group, u):
                c, i = u // TILES, u % TILES
                buf = pairs[:, u % 2, 0:PAIRS].rearrange("p (t f) -> p t f", f=FIELDS)
                fields = x_col[:, c % CHUNKS, i, :]
                one = fields[:, 0:FIELDS].unsqueeze(1).broadcast_to([P, SHIFTS, FIELDS])
                other = fields[:, SHIFT0:SHIFT0 + FIELDS]
                other = bass.AP(other.tensor, other.offset, [list(other.ap[0]), [1, SHIFTS], [1, FIELDS]])
                pool.wait_ge(x_col_ready, chunk_count(group, c + 1))
                if not (isinstance(group, int) and group == 0 and u < 2):
                    pool.wait_ge(pair_t_ready, tile_count(group, u - 1, 2))
                else:
                    pool.wait_ge(consts_ready, 1)
                nc.gpsimd.tensor_tensor(buf, one, other, ALU.mult).then_inc(pairs_ready, 1)

            def before():
                nc.gpsimd.memset(ident[:, :], 0.0).then_inc(consts_step, 1)
                nc.gpsimd.memset(own[:, :], 1.0).then_inc(consts_step, 1)
                nc.gpsimd.memset(pairs[:, :, PAIRS:], 0.0)
                pool.wait_ge(consts_step, 2)
                nc.gpsimd.affine_select(out=ident[:, :], in_=ident[:, :], compare_op=ALU.not_equal, fill=1.0,
                                        base=0, pattern=[[-1, P]], channel_multiplier=1)
                nc.gpsimd.affine_select(out=own[:, :], in_=own[:, :], compare_op=ALU.is_ge, fill=0.0,
                                        base=0, pattern=[[-EMB, SAMPLES]], channel_multiplier=1).then_inc(consts_step, 1)
                pool.wait_ge(consts_step, 3)
                nc.gpsimd.affine_select(out=own[:, :], in_=own[:, :], compare_op=ALU.is_ge, fill=0.0,
                                        base=EMB - 1, pattern=[[EMB, SAMPLES]], channel_multiplier=-1).then_inc(consts_step, 1)
                pool.wait_ge(consts_step, 4)
                nc.gpsimd.tensor_copy(x_diag[:, :, :, FIELDS],
                                      own[:, :].unsqueeze(1).broadcast_to([P, TILES, SAMPLES])).then_inc(consts_ready, 1)
                pool.wait_ge(ids_loaded, 16)
                gather(range(FIELDS))
                for u in range(TILES + 1):
                    pair_products(0, u)

            per_step = -(-FIELDS // 7)

            def step(group, t):
                c, i = t // TILES, t % TILES
                if FIRST <= t < FIRST + 7 and not is_last(group):
                    if t == FIRST:
                        pool.wait_ge(ids_loaded, at(group, 16, 32))
                        pool.wait_ge(field_t_ready, at(group, len(POS_FIELD_T), len(POS_FIELD_T)))
                pool.wait_ge(x_col_ready, chunk_count(group, c + 1))
                if not (isinstance(group, int) and group == 0 and t < TILES):
                    pool.wait_ge(pool_ready, tile_count(group, t - TILES + 1))
                nc.gpsimd.tensor_tensor(
                    x_diag[:, i, :, 0:FIELDS],
                    x_col[:, c % CHUNKS, i, 0:FIELDS].unsqueeze(1).broadcast_to([P, SAMPLES, FIELDS]),
                    own[:, :].unsqueeze(2).broadcast_to([P, SAMPLES, FIELDS]), ALU.mult).then_inc(x_diag_ready, 1)
                if FIRST <= t < FIRST + 7 and not is_last(group):
                    gather(range(FIELDS)[(t - FIRST) * per_step:(t - FIRST + 1) * per_step])
                if not (is_last(group) and t + TILES + 1 >= GROUP_TILES):
                    pair_products(group, t + TILES + 1)

            run(step, pool, before)

        @block.tensor
        def _(pe):
            def field_transposes(group, g):
                pe.wait_ge(consts_ready, 1)
                if g == 0:
                    pe.wait_ge(rows_loaded, at(group, 16 * FIELDS, 16 * FIELDS))
                    if not (isinstance(group, int) and group == 0):
                        pe.wait_ge(out1_saved, chunk_count(group, 3 - CHUNKS))
                else:
                    pe.wait_ge(field_t_copied, at(group, len(POS_FIELD_T), g))
                for d in range(4):
                    mm = pe.matmul(mid[0:FIELDS, d * P:(d + 1) * P], rows[:, :, 4 * g + d], ident[:, :],
                                   start=True, stop=True)
                mm.then_inc(field_t_ready, 1)

            def tile_transposes(group, c):
                pe.wait_ge(consts_ready, 1)
                if c == 0:
                    pe.wait_ge(field_t_copied, at(group, len(POS_FIELD_T), len(POS_FIELD_T)))
                elif isinstance(group, int) and group == 0 and c == 1:
                    pe.wait_ge(x_col_ready, 1)
                else:
                    pe.wait_ge(out1_saved, chunk_count(group, c - 1))
                for i in range(TILES):
                    cols = (c * TILES + i) * P
                    mm = pe.matmul(mid[:, i * FIELDS:(i + 1) * FIELDS], x_field[:, cols:cols + P],
                                   ident[0:FIELDS, 0:FIELDS], start=True, stop=True)
                mm.then_inc(tile_t_ready, 1)

            def pair_transposes(group, u, half):
                if half == 0:
                    pe.wait_ge(pairs_ready, tile_count(group, u + 1))
                if not (isinstance(group, int) and group == 0 and u == 0):
                    pe.wait_ge(pair_low, tile_count(group, u, 2) + (half - 1))
                for k in (range(0, 4), range(4, PAIR_BLOCKS))[half]:
                    mm = pe.transpose(pair_t[:, half, (k % 4) * P:(k % 4 + 1) * P],
                                      pairs[:, u % 2, k * P:(k + 1) * P], ident[:, :])
                mm.then_inc(pair_t_ready, 1)

            def cross1(group, c, blocks):
                if blocks[0] == 0:
                    pe.wait_ge(pair_low, tile_count(group, TILES * (c + 1), 2))
                    pe.wait_ge(x_col_ready, chunk_count(group, min(c + 2, CHUNKS) if is_last(group) else c + 2))
                    if isinstance(group, int) and group == 0 and c == 0:
                        pe.wait_ge(w0_ready, 1)
                for k in blocks:
                    rows_k = P if k < PAIR_BLOCKS - 1 else PAIR_REST
                    for a, b in ((w0_h, pair_h), (w0_l, pair_h), (w0_h, pair_l)):
                        mm = pe.matmul(mid[:, :], a[0:rows_k, k, :], b[0:rows_k, k, :],
                                       start=(k == 0 and a is w0_h and b is pair_h),
                                       stop=(k == PAIR_BLOCKS - 1 and b is pair_l))
                if blocks[-1] == PAIR_BLOCKS - 1:
                    mm.then_inc(cross1_ready, 1)

            def pool_columns(group, t):
                pe.wait_ge(c2_ready, tile_count(group, t + 1, 2))
                pe.wait_ge(x_diag_ready, tile_count(group, t + 1))
                if not is_start(group, t):
                    pe.wait_ge(pooled_saved, tile_count(group, t))
                if t == GROUP_TILES:
                    pe.wait_ge(out3_ready, at(group, 1, 1))
                n = SAMPLES * (FIELDS + 1)
                pe.matmul(pool_ps[:, 0:n], c2[:, t % 2, :],
                          x_diag[:, t % TILES, :, :].rearrange("p b f -> p (b f)"),
                          start=True, stop=True).then_inc(pool_ready, 1)

            def cross3(group):
                pe.wait_ge(pooled_saved, tile_count(group, GROUP_TILES))
                pe.wait_ge(w2_loaded, 16)
                for f in range(FIELDS):
                    mm = pe.matmul(pool_ps[:, 0:P], w2_sb[:, f * MAPS:(f + 1) * MAPS], pooled[:, f, :],
                                   start=(f == 0), stop=(f == FIELDS - 1))
                mm.then_inc(cross3_ready, 1)

            def tower1(group):
                pe.wait_ge(out3_ready, at(group, 1, 1))
                pe.wait_ge(out1_ready, at(group, 1, 1))
                pe.wait_ge(tower_loaded, 16 * 7)
                for j in range(MLP1 // P):
                    cols = slice(j * P, (j + 1) * P)
                    for k, z in enumerate((out1_done[:, :], pooled[:, FIELDS, :], out3[:, :])):
                        pe.matmul(mid[:, cols], wt1_sb[:, k, cols], z, start=(k == 0), stop=False)
                    mm = pe.matmul(mid[:, cols], wt1_d[:, cols], dense_sb[:, bass.ds(group * P, P)],
                                   start=False, stop=True)
                mm.then_inc(h1_ready, 1)

            def tower2(group):
                pe.wait_ge(h1_saved, at(group, 1, 1))
                for j in range(MLP2 // P):
                    cols = slice(j * P, (j + 1) * P)
                    for k in range(MLP1 // P):
                        mm = pe.matmul(mid[:, cols], wt2_sb[:, k, cols], h1[:, k, :],
                                       start=(k == 0), stop=(k == MLP1 // P - 1))
                mm.then_inc(h2_ready, 1)

            def tower3(group):
                pe.wait_ge(h2_saved, at(group, 1, 1))
                for k in range(MLP2 // P):
                    mm = pe.matmul(mid[0:1, 0:P], wt3_sb[:, k:k + 1], h2[:, k, :],
                                   start=(k == 0), stop=(k == MLP2 // P - 1))
                mm.then_inc(y_ready, 1)

            def before():
                for g in range(4):
                    field_transposes(0, g)
                tile_transposes(0, 0)
                tile_transposes(0, 1)
                for u in range(TILES):
                    pair_transposes(0, u, 0)
                    pair_transposes(0, u, 1)
                cross1(0, 0, range(PAIR_BLOCKS))

            def step(group, t):
                c, i = t // TILES, t % TILES
                for j in range(BANKS):
                    n = BANKS * t + j
                    if i == 0 and j == 0:
                        pe.wait_ge(c1_low, chunk_count(group, c + 1))
                        if is_start(group, t):
                            pe.wait_ge(w1_ready, 1)
                    if not (isinstance(group, int) and group == 0 and n < RING):
                        tb, jb = (n - RING) // BANKS, (n - RING) % BANKS
                        if jb in ACT_BANKS:
                            pe.wait_ge(act_bank_done, act_count(group, tb, ACT_BANKS.index(jb) + 1))
                        else:
                            pe.wait_ge(dve_unit_done, dve_count(group, tb, BANK_FIELDS * (DVE_BANKS.index(jb) + 1)))
                    fs = bank_fields(j)
                    cols = slice(fs[0] * MAPS, (fs[-1] + 1) * MAPS)
                    bank = prod[:, n % RING, 0:len(fs) * MAPS]
                    high = c1_h[:, c % 2, i * P:(i + 1) * P]
                    low = c1_l[:, c % 2, i * P:(i + 1) * P]
                    pe.matmul(bank, high, w1_h[:, cols], start=True, stop=False)
                    pe.matmul(bank, high, w1_l[:, cols], start=False, stop=False)
                    pe.matmul(bank, low, w1_h[:, cols], start=False, stop=True).then_inc(prod_ready, 1)

                    pos = BANKS * i + j
                    next_chunk = not (is_last(group) and c + 1 >= CHUNKS)
                    if next_chunk:
                        for u, halves in enumerate(POS_TRANSPOSE):
                            if pos in halves:
                                pair_transposes(group, TILES * (c + 1) + u, halves.index(pos))
                        if pos in POS_CROSS1:
                            cross1(group, c + 1, POS_CROSS1[pos])
                    if c % CHUNKS == 2 and pos in POS_FIELD_T and not is_last(group):
                        field_transposes(group + 1, POS_FIELD_T.index(pos))
                    if pos == POS_TILE_T and not (is_last(group) and c + 2 >= CHUNKS):
                        if t == GROUP_TILES + 2:
                            pe.wait_ge(y_saved, at(group, 1, 1))
                        tile_transposes_of(group, c + 2)
                    if j == POS_POOLED and not is_start(group, t):
                        pool_columns(group, t - 1)
                    if t == GROUP_TILES + 1 and j == 3:
                        cross3(group)
                    if t == GROUP_TILES + 1 and j == 6:
                        tower1(group)
                    if t == GROUP_TILES + 2 and j == 1:
                        tower2(group)
                    if t == GROUP_TILES + 2 and j == 4:
                        tower3(group)

            def tile_transposes_of(group, c):
                tile_transposes(group + c // CHUNKS, c % CHUNKS)

            run(step, pe, before)
            last = GROUPS - 1
            pool_columns(last, GROUP_TILES - 1)
            cross3(last)
            tower1(last)
            tower2(last)
            tower3(last)

        @block.scalar
        def _(act):
            def copy_fields(group, g):
                act.wait_ge(field_t_ready, at(group, 4, g + 1))
                nc.scalar.activation(
                    x_field[:, :].rearrange("f (b d) -> f d b", d=EMB)[:, 4 * g:4 * g + 4, :],
                    mid[0:FIELDS, :].rearrange("f (d b) -> f d b", b=P), ACT.Copy).then_inc(field_t_copied, 1)

            def copy_columns(group, c):
                act.wait_ge(tile_t_ready, chunk_count(group, c + 1))
                nc.scalar.activation(
                    x_col[:, c % CHUNKS, :, :].rearrange("p i (r f) -> p i r f", r=2),
                    mid[:, 0:TILES * FIELDS].rearrange("p (i f) -> p i f", f=FIELDS).unsqueeze(2)
                    .broadcast_to([P, TILES, 2, FIELDS]), ACT.Copy).then_inc(x_col_ready, 1)

            def pair_highs(group, u, half):
                act.wait_ge(pair_t_ready, tile_count(group, u, 2) + (half + 1))
                if u % TILES == 0 and half == 0 and not (isinstance(group, int) and group == 0 and u == 0):
                    act.wait_ge(cross1_ready, chunk_count(group, u // TILES))
                i, ks = u % TILES, (slice(0, 4), slice(4, PAIR_BLOCKS))[half]
                n = ks.stop - ks.start
                nc.scalar.activation(pair_h[:, ks, i * P:(i + 1) * P],
                                     pair_t[:, half, 0:n * P].rearrange("p (k n) -> p k n", n=P),
                                     ACT.Copy).then_inc(pair_high, 1)

            def c1_highs(group, c):
                act.wait_ge(cross1_ready, chunk_count(group, c + 1))
                nc.scalar.activation(c1_h[:, c % 2, :], mid[:, :], ACT.Copy).then_inc(c1_high, 1)

            def save_pooled(group, t):
                act.wait_ge(pool_ready, tile_count(group, t + 1))
                b = SAMPLES * (t % GROUP_TILES)
                nc.scalar.activation(
                    pooled[:, :, b:b + SAMPLES],
                    pool_ps[:, 0:SAMPLES * (FIELDS + 1)].rearrange("g (b f) -> g f b", b=SAMPLES),
                    ACT.Copy).then_inc(pooled_saved, 1)

            def store_y(group):
                act.wait_ge(y_saved, at(group, 1, 1))
                act.dma_start(out[:, bass.ds(group * P, P)], y_sb[:, :]).then_inc(y_stored, 16)

            def before():
                act.wait_ge(consts_ready, 1)
                nc.scalar.activation(warm[:, :], ident[:, 0:1], ACT.Copy)
                for g in range(4):
                    copy_fields(0, g)
                copy_columns(0, 0)
                copy_columns(0, 1)
                for u in range(TILES):
                    pair_highs(0, u, 0)
                    pair_highs(0, u, 1)
                c1_highs(0, 0)
                act.wait_ge(w0_ready, 1)

            def step(group, t):
                c, i = t // TILES, t % TILES
                for j in range(BANKS):
                    if j in ACT_BANKS:
                        if i == 0 and j == 0:
                            act.wait_ge(x_col_ready, chunk_count(group, c + 1))
                        if j == 0 and not (isinstance(group, int) and group == 0 and t < 2):
                            act.wait_ge(c2_ready, tile_count(group, t - 1, 2))
                        act.wait_ge(prod_ready, tile_count(group, t, BANKS) + (j + 1))
                        for f in bank_fields(j):
                            b = f % BANK_FIELDS
                            a = nc.scalar.activation(
                                terms[:, t % 2, ACT_SLOT[f], :],
                                prod[:, (BANKS * t + j) % RING, b * MAPS:(b + 1) * MAPS], ACT.Copy,
                                scale=x_col[:, c % CHUNKS, i, f:f + 1])
                        a.then_inc(act_bank_done, 1)
                    pos = BANKS * i + j - 1
                    next_chunk = not (is_last(group) and c + 1 >= CHUNKS)
                    if next_chunk:
                        for u, halves in enumerate(POS_TRANSPOSE):
                            if pos in halves:
                                pair_highs(group, TILES * (c + 1) + u, halves.index(pos))
                        if pos == max(POS_CROSS1):
                            c1_highs(group, c + 1)
                    if c % CHUNKS == 2 and pos in POS_FIELD_T and not is_last(group):
                        copy_fields(group + 1, POS_FIELD_T.index(pos))
                    if pos == POS_TILE_T and not (is_last(group) and c + 2 >= CHUNKS):
                        copy_columns(group + (c + 2) // CHUNKS, (c + 2) % CHUNKS)
                    if j == 1 and not (isinstance(group, int) and group == 0 and t < 2):
                        save_pooled(group, t - 2)
                    if t == GROUP_TILES + 2 and j == 9:
                        store_y(group)

            run(step, act, before)
            save_pooled(GROUPS - 1, GROUP_TILES - 2)
            save_pooled(GROUPS - 1, GROUP_TILES - 1)
            store_y(GROUPS - 1)

        @block.vector
        def _(dve):
            def pair_lows(group, u, half):
                dve.wait_ge(pair_high, tile_count(group, u, 2) + (half + 1))
                i, ks = u % TILES, (slice(0, 4), slice(4, PAIR_BLOCKS))[half]
                n = ks.stop - ks.start
                nc.vector.tensor_tensor(pair_l[:, ks, i * P:(i + 1) * P],
                                        pair_t[:, half, 0:n * P].rearrange("p (k n) -> p k n", n=P),
                                        pair_h[:, ks, i * P:(i + 1) * P].bitcast(F32),
                                        ALU.subtract).then_inc(pair_low, 1)

            def c1_lows(group, c):
                dve.wait_ge(c1_high, chunk_count(group, c + 1))
                nc.vector.tensor_tensor(c1_l[:, c % 2, :], mid[:, :], c1_h[:, c % 2, :].bitcast(F32),
                                        ALU.subtract).then_inc(c1_low, 1)
                q = c % CHUNKS
                if q == 0 and c > 0:
                    keep_out1(group)
                    dve.wait_ge(out1_ready, at(group, 1, 1))
                nc.vector.tensor_reduce(out1[:, q * CHUNK_SAMPLES:(q + 1) * CHUNK_SAMPLES],
                                        mid[:, :].rearrange("m (b d) -> m b d", d=EMB), AX_X,
                                        ALU.add).then_inc(out1_saved, 1)

            def keep_out1(group):
                dve.wait_ge(out1_saved, chunk_count(group, CHUNKS))
                nc.vector.tensor_copy(out1_done[:, :], out1[:, :]).then_inc(out1_ready, 1)

            def sum_terms(group, t, half):
                dve.wait_ge(act_bank_done, act_count(group, t + 1, 0))
                dve.wait_ge(dve_unit_done, dve_count(group, t + 1, 0))
                if not (isinstance(group, int) and group == 0 and t < 2):
                    dve.wait_ge(pool_ready, tile_count(group, t - 1))
                cols = slice(half * MAPS // 2, (half + 1) * MAPS // 2)
                nc.vector.tensor_reduce(c2[:, t % 2, cols],
                                        terms[:, t % 2, :, cols].rearrange("p s m -> p m s"), AX_X,
                                        ALU.add).then_inc(c2_ready, 1)

            def save_out3(group):
                dve.wait_ge(cross3_ready, at(group, 1, 1))
                nc.vector.tensor_copy(out3[:, :], pool_ps[:, 0:P]).then_inc(out3_ready, 1)

            def relu(ready, saved, dst, bias, n, group):
                dve.wait_ge(ready, at(group, 1, 1))
                for j in range(n):
                    v = nc.vector.tensor_scalar(dst[:, j, :], mid[:, j * P:(j + 1) * P], bias[:, j:j + 1], 0.0,
                                                ALU.add, ALU.max)
                v.then_inc(saved, 1)

            def save_y(group):
                dve.wait_ge(y_free, at(group, 1, 1))
                dve.wait_ge(y_ready, at(group, 1, 1))
                nc.vector.tensor_copy(y_sb[:, :], mid[0:1, 0:P]).then_inc(y_saved, 1)

            def before():
                nc.vector.memset(y_sb[:, :], 0.0).then_inc(y_free, 1)
                nc.vector.memset(w0_b_raw[:, CROSS // P:PAIR_BLOCKS, :], 0.0).then_inc(w0_zeroed, 1)
                full = PAIR_BLOCKS - 1
                dve.wait_ge(w0_zeroed, 1)
                dve.wait_ge(w0_loaded, 16 * 4)
                parts = (slice(0, P), slice(0, full)), (slice(0, PAIR_REST), slice(full, PAIR_BLOCKS))
                for r, k in parts:
                    nc.vector.tensor_tensor(w0_sum[r, k, :], w0_a_raw[r, k, :], w0_b_raw[r, k, :],
                                            ALU.add).then_inc(w0_summed, 1)
                dve.wait_ge(w0_summed, 2)
                for r, k in parts:
                    nc.vector.tensor_copy(w0_h[r, k, :], w0_sum[r, k, :]).then_inc(w0_high, 1)
                dve.wait_ge(w0_high, 2)
                for r, k in parts:
                    v = nc.vector.tensor_tensor(w0_l[r, k, :], w0_sum[r, k, :], w0_h[r, k, :].bitcast(F32),
                                                ALU.subtract)
                v.then_inc(w0_ready, 1)
                dve.wait_ge(w1_loaded, 16)
                nc.vector.tensor_copy(w1_h[:, :], w1_raw).then_inc(w1_high, 1)
                dve.wait_ge(w1_high, 1)
                nc.vector.tensor_tensor(w1_l[:, :], w1_raw, w1_h[:, :].bitcast(F32),
                                        ALU.subtract).then_inc(w1_ready, 1)
                for u in range(TILES):
                    pair_lows(0, u, 0)
                    pair_lows(0, u, 1)
                c1_lows(0, 0)

            def step(group, t):
                c, i = t // TILES, t % TILES
                for j in range(BANKS):
                    if j in DVE_BANKS:
                        if j == DVE_BANKS[0]:
                            dve.wait_ge(x_col_ready, chunk_count(group, c + 1))
                        dve.wait_ge(prod_ready, tile_count(group, t, BANKS) + (j + 1))
                        for f in bank_fields(j):
                            b, n = f % BANK_FIELDS, DVE_ORDER.index(f)
                            src = prod[:, (BANKS * t + j) % RING, b * MAPS:(b + 1) * MAPS]
                            x = x_col[:, c % CHUNKS, i, f:f + 1]
                            acc = terms[:, t % 2, SLOTS - 2 + n % 2, :]
                            if n < 2:
                                v = nc.vector.tensor_scalar(acc, src, x, None, ALU.mult)
                            else:
                                dve.wait_ge(dve_unit_done, dve_count(group, t, n - 1))
                                v = nc.vector.scalar_tensor_tensor(out=acc, in0=src, scalar=x, in1=acc,
                                                                   op0=ALU.mult, op1=ALU.add)
                            v.then_inc(dve_unit_done, 1)
                    if j == 1 and not is_start(group, t):
                        sum_terms(group, t - 1, 0)
                    if j == 5 and not is_start(group, t):
                        sum_terms(group, t - 1, 1)
                    pos = BANKS * i + j - 2
                    next_chunk = not (is_last(group) and c + 1 >= CHUNKS)
                    if next_chunk:
                        for u, halves in enumerate(POS_TRANSPOSE):
                            if pos in halves:
                                pair_lows(group, TILES * (c + 1) + u, halves.index(pos))
                        if pos == max(POS_CROSS1):
                            c1_lows(group, c + 1)
                    if t == GROUP_TILES + 1 and j == 4:
                        save_out3(group)
                    if t == GROUP_TILES + 1 and j == 8:
                        relu(h1_ready, h1_saved, h1, bt1_sb, MLP1 // P, group)
                    if t == GROUP_TILES + 2 and j == 2:
                        relu(h2_ready, h2_saved, h2, bt2_sb, MLP2 // P, group)
                    if t == GROUP_TILES + 2 and j == 6:
                        save_y(group)

            run(step, dve, before)
            last = GROUPS - 1
            sum_terms(last, GROUP_TILES - 1, 0)
            sum_terms(last, GROUP_TILES - 1, 1)
            keep_out1(last)
            save_out3(last)
            relu(h1_ready, h1_saved, h1, bt1_sb, MLP1 // P, last)
            relu(h2_ready, h2_saved, h2, bt2_sb, MLP2 // P, last)
            save_y(last)


def kernel(**inputs):
    import concourse.bacc as bacc
    from concourse.bass_utils import run_bass_kernel_spmd

    f = np.tile(np.arange(FIELDS), SHIFTS)
    g = (f + SHIFT0 + np.repeat(np.arange(SHIFTS), FIELDS)) % FIELDS
    w0 = np.asarray(inputs["L0_rec_f0"])
    arrays = {
        "ids": np.asarray(inputs["ids"]),
        "dense_t": np.asarray(inputs["dense_ctx"]).T,
        "w0_a": w0[f * FIELDS + g],
        "w0_b": w0[(g * FIELDS + f)[:CROSS]],
        "w1": inputs["L0_rec_f1"],
        "w2": inputs["L0_rec_f2"],
        "wt1": inputs["W_top1"],
        "bt1": np.asarray(inputs["b_top1"]).reshape(MLP1 // P, P).T,
        "wt2": inputs["W_top2"],
        "bt2": np.asarray(inputs["b_top2"]).reshape(MLP2 // P, P).T,
        "wt3": np.asarray(inputs["W_top3"]).reshape(MLP2 // P, P).T,
    }
    for n in range(FIELDS):
        arrays[f"tbl_{n}"] = inputs[f"tbl_{n}"]
    arrays = {n: np.ascontiguousarray(a) for n, a in arrays.items()}

    nc = bacc.Bacc("TRN2", target_bir_lowering=False, num_devices=1)
    ap = {n: nc.dram_tensor(n, a.shape, mybir.dt.from_np(a.dtype), kind="ExternalInput").ap()
          for n, a in arrays.items()}
    out = nc.dram_tensor("y", (1, BATCH), F32, kind="ExternalOutput").ap()
    cin_program(nc, ap["ids"], [ap[f"tbl_{n}"] for n in range(FIELDS)], ap["dense_t"], ap["w0_a"], ap["w0_b"],
                ap["w1"], ap["w2"], ap["wt1"], ap["bt1"], ap["wt2"], ap["bt2"], ap["wt3"], out)
    result = run_bass_kernel_spmd(nc, [arrays], core_ids=[0])
    return result.results[0]["y"].reshape(BATCH, 1)
```

```python
from contextlib import ExitStack

import numpy as np

import concourse.bass as bass
from concourse import mybir
from concourse.alu_op_type import AluOpType as ALU

F32 = mybir.dt.float32
F32R = mybir.dt.float32r
I32 = mybir.dt.int32
ACT = mybir.ActivationFunctionType
AX_X = mybir.AxisListType.X

FIELDS = 39
EMB = 16
BATCH = 512
MAPS = 128
P = 128

SAMPLES = P // EMB
TILES = 4
CHUNKS = 4
GROUPS = BATCH // P
GROUP_TILES = TILES * CHUNKS
CHUNK = TILES * P
CHUNK_SAMPLES = TILES * SAMPLES

SHIFTS = (FIELDS + 1) // 2
SHIFT0 = FIELDS - SHIFTS + 1
PAIRS = SHIFTS * FIELDS
CROSS = PAIRS - FIELDS
BLOCK_SHIFTS = P // FIELDS
BLOCK = BLOCK_SHIFTS * FIELDS
PAIR_BLOCKS = -(-SHIFTS // BLOCK_SHIFTS)


def block_shifts(k):
    return range(BLOCK_SHIFTS * k, min(BLOCK_SHIFTS * (k + 1), SHIFTS))


def block_rows(k):
    return len(block_shifts(k)) * FIELDS


BANK_FIELDS = 4
BANKS = -(-FIELDS // BANK_FIELDS)
RING = 5
ACT_BANKS = (0, 2, 3, 5, 6, 8, 9)
DVE_BANKS = (1, 4, 7)
assert sorted(ACT_BANKS + DVE_BANKS) == list(range(BANKS))


def bank_fields(j):
    return range(BANK_FIELDS * j, min(BANK_FIELDS * (j + 1), FIELDS))


ACT_SLOT = {f: n for n, f in enumerate(f for j in ACT_BANKS for f in bank_fields(j))}
DVE_ORDER = [f for j in DVE_BANKS for f in bank_fields(j)]
SLOTS = len(ACT_SLOT) + 2

POS_HIGH = {4 + 4 * k: k for k in range(PAIR_BLOCKS)}
POS_LOW = {6 + 4 * k: k for k in range(PAIR_BLOCKS)}
POS_CROSS1 = {10 + 4 * k: k for k in range(PAIR_BLOCKS)}
POS_C1_HIGH = 35
POS_C1_LOW = 37
POS_TILE_T = 5
POS_ROWS = 28
POS_FIELD_T = (30, 32, 34, 36)
POOL_PAIRS = ((0, 1, 2), (3, 4), (5, 6), ())
POOL_LOWS = ((0, 1), (2, 3), (4, 5), (6,))
POOL_LOW_CHUNKS = (0, 1)
POS_POOLED = 9
STEP_CROSS3 = 17
CROSS3_BANKS = (3, 4, 5, 6, 7, 8)
STEP_TOWER = 18
FIRST = 4
GATHER_STEPS = 7

MLP1 = 512
MLP2 = 256
DENSE = 16
K_MLP1 = 3


def at(group, per_group, const):
    return group * per_group + const


def cin_program(nc, ids, tables, dense_t, w0_a, w0_b, w1, w2, wt1, bt1, wt2, bt2, wt3, out):
    with ExitStack() as ctx:
        def sb(name, shape, dt=F32):
            return ctx.enter_context(nc.sbuf_tensor(name, shape, dt))

        def sem(name):
            return ctx.enter_context(nc.semaphore(name))

        prod = ctx.enter_context(nc.psum_tensor("prod", [P, RING, 512], F32))
        aux = ctx.enter_context(nc.psum_tensor("aux", [P, 512], F32))
        mid = ctx.enter_context(nc.psum_tensor("mid", [P, 512], F32))
        pool_ps = ctx.enter_context(nc.psum_tensor("pool_ps", [P, 512], F32))

        ids_sb = sb("ids_sb", [P, FIELDS], I32)
        rows = sb("rows", [P, 2 * FIELDS, EMB])
        x_field = sb("x_field", [2 * FIELDS, P * EMB])
        x_col = sb("x_col", [P, CHUNKS, TILES, FIELDS])
        pair_one = sb("pair_one", [BLOCK, CHUNK])
        pairs = sb("pairs", [BLOCK, PAIR_BLOCKS, CHUNK])
        pair_h = sb("pair_h", [BLOCK, PAIR_BLOCKS, CHUNK], F32R)
        pair_l = sb("pair_l", [BLOCK, PAIR_BLOCKS, CHUNK], F32R)
        w0_h = sb("w0_h", [BLOCK, PAIR_BLOCKS, MAPS], F32R)
        w0_l = sb("w0_l", [BLOCK, PAIR_BLOCKS, MAPS], F32R)
        w1_h = sb("w1_h", [P, FIELDS * MAPS], F32R)
        w1_l = sb("w1_l", [P, FIELDS * MAPS], F32R)
        w2_sb = sb("w2_sb", [P, FIELDS * MAPS])
        c1_h = sb("c1_h", [P, 2, CHUNK], F32R)
        c1_l = sb("c1_l", [P, 2, CHUNK], F32R)
        terms = sb("terms", [P, 2, SLOTS, MAPS])
        c2 = sb("c2", [P, 2, MAPS])
        x_diag = sb("x_diag", [P, 2, SAMPLES, FIELDS + 1])
        pooled = sb("pooled", [P, FIELDS + 1, P])
        out1 = sb("out1", [P, P])
        out1_done = sb("out1_done", [P, P])
        out2 = sb("out2", [P, P])
        out3 = sb("out3", [P, P])
        dense_sb = sb("dense_sb", [DENSE, BATCH])
        wt1_sb = sb("wt1_sb", [P, K_MLP1, MLP1])
        wt1_d = sb("wt1_d", [DENSE, MLP1])
        wt2_sb = sb("wt2_sb", [P, MLP1 // P, MLP2])
        wt3_sb = sb("wt3_sb", [P, MLP2 // P])
        bt1_sb = sb("bt1_sb", [P, MLP1 // P])
        bt2_sb = sb("bt2_sb", [P, MLP2 // P])
        h1 = sb("h1", [P, MLP1 // P, P])
        h2 = sb("h2", [P, MLP2 // P, P])
        y_sb = sb("y_sb", [1, BATCH])
        ident = sb("ident", [P, P])
        own = sb("own", [P, SAMPLES])
        warm = sb("warm", [P, 1])

        w1_raw = pooled[:, :, :].rearrange("p f b -> p (f b)")[:, 0:FIELDS * MAPS]
        w0_a_raw = terms[:, 0, 0:PAIR_BLOCKS, :]
        w0_b_raw = terms[:, 0, PAIR_BLOCKS:2 * PAIR_BLOCKS, :]
        w0_sum = terms[:, 0, 2 * PAIR_BLOCKS:3 * PAIR_BLOCKS, :]

        ids_loaded = sem("ids_loaded")
        w0_loaded = sem("w0_loaded")
        w1_loaded = sem("w1_loaded")
        w2_loaded = sem("w2_loaded")
        tower_loaded = sem("tower_loaded")
        rows_loaded = sem("rows_loaded")
        rows_doubled = sem("rows_doubled")
        consts_step = sem("consts_step")
        consts_ready = sem("consts_ready")
        w0_zeroed = sem("w0_zeroed")
        w0_summed = sem("w0_summed")
        w0_high = sem("w0_high")
        w0_ready = sem("w0_ready")
        w1_high = sem("w1_high")
        w1_ready = sem("w1_ready")
        field_t_ready = sem("field_t_ready")
        field_t_copied = sem("field_t_copied")
        tile_t_ready = sem("tile_t_ready")
        x_col_ready = sem("x_col_ready")
        one_loaded = sem("one_loaded")
        other_loaded = [sem(f"other_loaded_{k}") for k in range(PAIR_BLOCKS)]
        x_field_read = sem("x_field_read")
        first_pairs_ready = sem("first_pairs_ready")
        first_pairs_low = sem("first_pairs_low")
        pairs_ready = sem("pairs_ready")
        pair_high = sem("pair_high")
        pool_pair_low = sem("pool_pair_low")
        dve_pair_low = sem("dve_pair_low")
        cross1_ready = sem("cross1_ready")
        c1_high = sem("c1_high")
        c1_low = sem("c1_low")
        out1_saved = sem("out1_saved")
        out1_ready = sem("out1_ready")
        prod_ready = sem("prod_ready")
        act_bank_done = sem("act_bank_done")
        dve_unit_done = sem("dve_unit_done")
        c2_ready = sem("c2_ready")
        x_diag_ready = sem("x_diag_ready")
        pool_ready = sem("pool_ready")
        pooled_saved = sem("pooled_saved")
        cross3_ready = sem("cross3_ready")
        out2_ready = sem("out2_ready")
        out3_ready = sem("out3_ready")
        h1_ready = sem("h1_ready")
        h1_saved = sem("h1_saved")
        h2_ready = sem("h2_ready")
        h2_saved = sem("h2_saved")
        y_ready = sem("y_ready")
        y_saved = sem("y_saved")
        y_stored = sem("y_stored")

        def act_count(group, t, n):
            return at(group, len(ACT_BANKS) * GROUP_TILES, len(ACT_BANKS) * t + n)

        def dve_count(group, t, n):
            return at(group, len(DVE_ORDER) * GROUP_TILES, len(DVE_ORDER) * t + n)

        def tile_count(group, t, per_tile=1):
            return at(group, per_tile * GROUP_TILES, per_tile * t)

        def chunk_count(group, c, per_chunk=1):
            return at(group, per_chunk * CHUNKS, per_chunk * c)

        def is_first(group, c):
            return isinstance(group, int) and group == 0 and c == 0

        def wait_pairs(eng, group, c, k):
            if is_first(group, c):
                eng.wait_ge(first_pairs_ready, k + 1)
            else:
                eng.wait_ge(pairs_ready, chunk_count(group, c, PAIR_BLOCKS) + (k + 1 - PAIR_BLOCKS))

        def pool_makes_low(c):
            return c % CHUNKS in POOL_LOW_CHUNKS

        def wait_pair_low(eng, group, c, k):
            if is_first(group, c):
                eng.wait_ge(first_pairs_low, k + 1)
                return
            q, per_group = c % CHUNKS, len(POOL_LOW_CHUNKS) * PAIR_BLOCKS
            done = c // CHUNKS * per_group + k + 1
            if pool_makes_low(c):
                eng.wait_ge(pool_pair_low, at(group, per_group, done + POOL_LOW_CHUNKS.index(q) * PAIR_BLOCKS - PAIR_BLOCKS))
            else:
                eng.wait_ge(dve_pair_low, at(group, per_group, done + (q - len(POOL_LOW_CHUNKS)) * PAIR_BLOCKS))

        def make_pairs(ns, k, done):
            n = block_rows(k)
            ns.tensor_tensor(pairs[0:n, k, :], pairs[0:n, k, :], pair_one[0:n, :], ALU.mult).then_inc(done, 1)

        def make_pair_low(ns, k, done):
            n = block_rows(k)
            ns.tensor_tensor(pair_l[0:n, k, :], pairs[0:n, k, :], pair_h[0:n, k, :].bitcast(F32),
                             ALU.subtract).then_inc(done, 1)

        def run(step, eng, before):
            before()
            for t in range(FIRST):
                step(0, t)
            with eng.Fori(0, GROUPS - 1) as group:
                for t in range(FIRST, FIRST + GROUP_TILES):
                    step(group, t)
            for t in range(FIRST, GROUP_TILES):
                step(GROUPS - 1, t)

        def is_last(group):
            return isinstance(group, int) and group == GROUPS - 1

        def is_start(group, t):
            return isinstance(group, int) and group == 0 and t == 0

        block = ctx.enter_context(nc.Block())

        @block.sync
        def _(sp):
            sp.dma_start(ids_sb[:, :], ids[0:P, :]).then_inc(ids_loaded, 16)
            full, rest = (PAIR_BLOCKS - 1) * BLOCK, block_rows(PAIR_BLOCKS - 1)
            sp.dma_start(w0_a_raw[0:BLOCK, 0:PAIR_BLOCKS - 1, :],
                         w0_a[0:full, :].rearrange("(k p) m -> p k m", p=BLOCK)).then_inc(w0_loaded, 16)
            sp.dma_start(w0_a_raw[0:rest, PAIR_BLOCKS - 1, :], w0_a[full:PAIRS, :]).then_inc(w0_loaded, 16)
            sp.dma_start(w0_b_raw[0:BLOCK, 0:PAIR_BLOCKS - 1, :],
                         w0_b[0:full, :].rearrange("(k p) m -> p k m", p=BLOCK)).then_inc(w0_loaded, 16)
            sp.wait_ge(w0_zeroed, 1)
            sp.dma_start(w0_b_raw[0:CROSS - full, PAIR_BLOCKS - 1, :], w0_b[full:CROSS, :]).then_inc(w0_loaded, 16)
            sp.dma_start(w1_raw.rearrange("g (f m) -> g f m", m=MAPS),
                         w1.rearrange("(f g) m -> g f m", g=MAPS)).then_inc(w1_loaded, 16)
            sp.dma_start(w2_sb[:, :].rearrange("g (f m) -> g f m", m=MAPS),
                         w2.rearrange("(f g) m -> g f m", g=MAPS)).then_inc(w2_loaded, 16)
            sp.dma_start(wt1_sb[:, :, :], wt1[0:K_MLP1 * P, :].rearrange("(k p) m -> p k m", p=P)).then_inc(tower_loaded, 16)
            sp.dma_start(wt1_d[:, :], wt1[K_MLP1 * P:, :]).then_inc(tower_loaded, 16)
            sp.dma_start(wt2_sb[:, :, :], wt2.rearrange("(k p) m -> p k m", p=P)).then_inc(tower_loaded, 16)
            sp.dma_start(wt3_sb[:, :], wt3).then_inc(tower_loaded, 16)
            sp.dma_start(bt1_sb[:, :], bt1).then_inc(tower_loaded, 16)
            sp.dma_start(bt2_sb[:, :], bt2).then_inc(tower_loaded, 16)
            sp.dma_start(dense_sb[:, :], dense_t).then_inc(tower_loaded, 16)

            def spread_fields(group, c):
                cols = slice((c % CHUNKS) * CHUNK, (c % CHUNKS + 1) * CHUNK)
                if not is_first(group, c):
                    wait_pairs(sp, group, c - 1, PAIR_BLOCKS - 1)
                if c % CHUNKS == 0:
                    sp.wait_ge(field_t_copied, at(group, len(POS_FIELD_T), (c // CHUNKS + 1) * len(POS_FIELD_T)))
                for r in range(BLOCK_SHIFTS):
                    sp.dma_start(pair_one[r * FIELDS:(r + 1) * FIELDS, :],
                                 x_field[0:FIELDS, cols]).then_inc(one_loaded, 16)
                for k in range(PAIR_BLOCKS):
                    if not is_first(group, c):
                        wait_pair_low(sp, group, c - 1, k)
                    for r, t in enumerate(block_shifts(k)):
                        sp.dma_start(pairs[r * FIELDS:(r + 1) * FIELDS, k, :],
                                     x_field[SHIFT0 + t:SHIFT0 + t + FIELDS, cols]).then_inc(other_loaded[k], 16)

            def wait_spread(group, c):
                sp.wait_ge(one_loaded, chunk_count(group, c + 1, 16 * BLOCK_SHIFTS))
                for k in range(PAIR_BLOCKS):
                    sp.wait_ge(other_loaded[k], chunk_count(group, c + 1, 16 * len(block_shifts(k))))

            spread_fields(0, 0)
            spread_fields(0, 1)
            with sp.Fori(0, GROUPS - 1) as group:
                sp.wait_ge(rows_loaded, at(group, 16 * FIELDS, 16 * FIELDS))
                sp.dma_start(ids_sb[:, :], ids[bass.ds(group * P + P, P), :]).then_inc(ids_loaded, 16)
                for c in range(2, CHUNKS):
                    spread_fields(group, c)
                wait_spread(group, CHUNKS - 1)
                sp.sem_inc(x_field_read, 1)
                for c in range(CHUNKS, CHUNKS + 2):
                    spread_fields(group, c)
            for c in range(2, CHUNKS):
                spread_fields(GROUPS - 1, c)
            sp.wait_ge(y_saved, GROUPS)
            sp.dma_start(out, y_sb[:, :]).then_inc(y_stored, 16)
            sp.wait_ge(y_stored, 16)

        @block.gpsimd
        def _(pool):
            def gather(fields):
                for f in fields:
                    nc.gpsimd.indirect_dma_start(
                        rows[:, f, :], None, tables[f],
                        bass.IndirectOffsetOnAxis(ap=ids_sb[:, f:f + 1], axis=0)).then_inc(rows_loaded, 16)

            def products(group, c, k):
                if k == 0:
                    pool.wait_ge(one_loaded, chunk_count(group, c + 1, 16 * BLOCK_SHIFTS))
                pool.wait_ge(other_loaded[k], chunk_count(group, c + 1, 16 * len(block_shifts(k))))
                make_pairs(nc.gpsimd, k, pairs_ready)

            def lows(group, c, k):
                wait_pairs(pool, group, c, k)
                pool.wait_ge(pair_high, chunk_count(group, c, PAIR_BLOCKS) + (k + 1))
                if k == 0:
                    pool.wait_ge(cross1_ready, chunk_count(group, c))
                make_pair_low(nc.gpsimd, k, pool_pair_low)

            def before():
                nc.gpsimd.memset(ident[:, :], 0.0).then_inc(consts_step, 1)
                nc.gpsimd.memset(own[:, :], 1.0).then_inc(consts_step, 1)
                pool.wait_ge(consts_step, 2)
                nc.gpsimd.affine_select(out=ident[:, :], in_=ident[:, :], compare_op=ALU.not_equal, fill=1.0,
                                        base=0, pattern=[[-1, P]], channel_multiplier=1)
                nc.gpsimd.affine_select(out=own[:, :], in_=own[:, :], compare_op=ALU.is_ge, fill=0.0,
                                        base=0, pattern=[[-EMB, SAMPLES]], channel_multiplier=1).then_inc(consts_step, 1)
                pool.wait_ge(consts_step, 3)
                nc.gpsimd.affine_select(out=own[:, :], in_=own[:, :], compare_op=ALU.is_ge, fill=0.0,
                                        base=EMB - 1, pattern=[[EMB, SAMPLES]], channel_multiplier=-1).then_inc(consts_step, 1)
                pool.wait_ge(consts_step, 4)
                nc.gpsimd.tensor_copy(x_diag[:, :, :, FIELDS],
                                      own[:, :].unsqueeze(1).broadcast_to([P, 2, SAMPLES])).then_inc(consts_ready, 1)
                pool.wait_ge(ids_loaded, 16)
                gather(range(FIELDS))

            per_step = -(-FIELDS // GATHER_STEPS)

            def step(group, t):
                c, i = t // TILES, t % TILES
                gathers = FIRST <= t < FIRST + GATHER_STEPS and not is_last(group)
                if gathers and t == FIRST:
                    pool.wait_ge(ids_loaded, at(group, 16, 32))
                    pool.wait_ge(field_t_ready, at(group, len(POS_FIELD_T), len(POS_FIELD_T)))
                pool.wait_ge(x_col_ready, chunk_count(group, c + 1))
                if not (isinstance(group, int) and group == 0 and t < 2):
                    pool.wait_ge(pool_ready, tile_count(group, t - 1))
                nc.gpsimd.tensor_tensor(
                    x_diag[:, t % 2, :, 0:FIELDS],
                    x_col[:, c % CHUNKS, i, 0:FIELDS].unsqueeze(1).broadcast_to([P, SAMPLES, FIELDS]),
                    own[:, :].unsqueeze(2).broadcast_to([P, SAMPLES, FIELDS]), ALU.mult).then_inc(x_diag_ready, 1)
                if not (is_last(group) and c + 1 >= CHUNKS):
                    for k in POOL_PAIRS[i]:
                        products(group, c + 1, k)
                    for k in POOL_LOWS[i] if pool_makes_low(c + 1) else ():
                        lows(group, c + 1, k)
                if gathers:
                    gather(range(FIELDS)[(t - FIRST) * per_step:(t - FIRST + 1) * per_step])

            run(step, pool, before)

        @block.tensor
        def _(pe):
            def field_transposes(group, g, bank):
                pe.wait_ge(consts_ready, 1)
                if g == 0:
                    pe.wait_ge(rows_doubled, at(group, 1, 1))
                    if not (isinstance(group, int) and group == 0):
                        pe.wait_ge(x_col_ready, chunk_count(group, 0))
                elif bank is aux:
                    pe.wait_ge(field_t_copied, at(group, len(POS_FIELD_T), g))
                for d in range(4):
                    mm = pe.matmul(bank[0:2 * FIELDS, d * P:(d + 1) * P], rows[:, :, 4 * g + d], ident[:, :],
                                   start=True, stop=True)
                mm.then_inc(field_t_ready, 1)

            def tile_transposes(group, c):
                pe.wait_ge(consts_ready, 1)
                if c % CHUNKS == 0:
                    pe.wait_ge(field_t_copied, at(group, len(POS_FIELD_T), (c // CHUNKS + 1) * len(POS_FIELD_T)))
                if not is_first(group, c):
                    pe.wait_ge(x_col_ready, chunk_count(group, c))
                for i in range(TILES):
                    cols = (c % CHUNKS * TILES + i) * P
                    mm = pe.matmul(aux[:, i * FIELDS:(i + 1) * FIELDS], x_field[0:FIELDS, cols:cols + P],
                                   ident[0:FIELDS, 0:FIELDS], start=True, stop=True)
                mm.then_inc(tile_t_ready, 1)

            def cross1(group, c, k):
                if k == 0:
                    if is_first(group, c):
                        pe.wait_ge(w0_ready, 1)
                    else:
                        pe.wait_ge(out1_saved, chunk_count(group, c))
                wait_pair_low(pe, group, c, k)
                n = block_rows(k)
                for a, b in ((w0_h, pair_h), (w0_l, pair_h), (w0_h, pair_l)):
                    mm = pe.matmul(mid[:, :], a[0:n, k, :], b[0:n, k, :],
                                   start=(k == 0 and a is w0_h and b is pair_h),
                                   stop=(k == PAIR_BLOCKS - 1 and b is pair_l))
                if k == PAIR_BLOCKS - 1:
                    mm.then_inc(cross1_ready, 1)

            def pool_columns(group, t):
                pe.wait_ge(c2_ready, tile_count(group, t + 1, 2))
                pe.wait_ge(x_diag_ready, tile_count(group, t + 1))
                if not is_start(group, t):
                    pe.wait_ge(pooled_saved, tile_count(group, t))
                n = SAMPLES * (FIELDS + 1)
                pe.matmul(pool_ps[:, 0:n], c2[:, t % 2, :],
                          x_diag[:, t % 2, :, :].rearrange("p b f -> p (b f)"),
                          start=True, stop=True).then_inc(pool_ready, 1)

            def cross3(group, fields):
                if fields[0] == 0:
                    pe.wait_ge(pooled_saved, tile_count(group, GROUP_TILES))
                    pe.wait_ge(w2_loaded, 16)
                for f in fields:
                    mm = pe.matmul(aux[:, 0:P], w2_sb[:, f * MAPS:(f + 1) * MAPS], pooled[:, f, :],
                                   start=(f == 0), stop=(f == FIELDS - 1))
                if fields[-1] == FIELDS - 1:
                    mm.then_inc(cross3_ready, 1)

            def tower1(group, j):
                if j == 0:
                    pe.wait_ge(out3_ready, at(group, 1, 1))
                    pe.wait_ge(out1_ready, at(group, 1, 1))
                    pe.wait_ge(out2_ready, at(group, 1, 1))
                    pe.wait_ge(tower_loaded, 16 * 7)
                cols = slice(j * P, (j + 1) * P)
                for k, z in enumerate((out1_done[:, :], out2[:, :], out3[:, :])):
                    pe.matmul(aux[:, cols], wt1_sb[:, k, cols], z, start=(k == 0), stop=False)
                mm = pe.matmul(aux[:, cols], wt1_d[:, cols], dense_sb[:, bass.ds(group * P, P)],
                               start=False, stop=True)
                if j == MLP1 // P - 1:
                    mm.then_inc(h1_ready, 1)

            def tower2(group):
                pe.wait_ge(h1_saved, at(group, 1, 1))
                for j in range(MLP2 // P):
                    cols = slice(j * P, (j + 1) * P)
                    for k in range(MLP1 // P):
                        mm = pe.matmul(aux[:, cols], wt2_sb[:, k, cols], h1[:, k, :],
                                       start=(k == 0), stop=(k == MLP1 // P - 1))
                mm.then_inc(h2_ready, 1)

            def tower3(group):
                pe.wait_ge(h2_saved, at(group, 1, 1))
                for k in range(MLP2 // P):
                    mm = pe.matmul(aux[0:1, 0:P], wt3_sb[:, k:k + 1], h2[:, k, :],
                                   start=(k == 0), stop=(k == MLP2 // P - 1))
                mm.then_inc(y_ready, 1)

            def before():
                for g in range(4):
                    field_transposes(0, g, prod[:, g, :])
                tile_transposes(0, 0)
                for k in range(PAIR_BLOCKS):
                    cross1(0, 0, k)

            cross3_step = -(-FIELDS // len(CROSS3_BANKS))

            def step(group, t):
                c, i = t // TILES, t % TILES
                for j in range(BANKS):
                    n = BANKS * t + j
                    if i == 0 and j == 0:
                        pe.wait_ge(c1_low, chunk_count(group, c + 1))
                        if is_start(group, t):
                            pe.wait_ge(w1_ready, 1)
                    if not (isinstance(group, int) and group == 0 and n < RING):
                        tb, jb = (n - RING) // BANKS, (n - RING) % BANKS
                        if jb in ACT_BANKS:
                            pe.wait_ge(act_bank_done, act_count(group, tb, ACT_BANKS.index(jb) + 1))
                        else:
                            pe.wait_ge(dve_unit_done, dve_count(group, tb, BANK_FIELDS * (DVE_BANKS.index(jb) + 1)))
                    fs = bank_fields(j)
                    cols = slice(fs[0] * MAPS, (fs[-1] + 1) * MAPS)
                    bank = prod[:, n % RING, 0:len(fs) * MAPS]
                    high = c1_h[:, c % 2, i * P:(i + 1) * P]
                    low = c1_l[:, c % 2, i * P:(i + 1) * P]
                    pe.matmul(bank, high, w1_h[:, cols], start=True, stop=False)
                    pe.matmul(bank, high, w1_l[:, cols], start=False, stop=False)
                    pe.matmul(bank, low, w1_h[:, cols], start=False, stop=True).then_inc(prod_ready, 1)

                    pos = BANKS * i + j
                    next_chunk = not (is_last(group) and c + 1 >= CHUNKS)
                    if next_chunk:
                        if pos in POS_CROSS1:
                            cross1(group, c + 1, POS_CROSS1[pos])
                        if pos == POS_TILE_T:
                            tile_transposes(group, c + 1)
                    if c % CHUNKS == 2 and pos in POS_FIELD_T and not is_last(group):
                        field_transposes(group + 1, POS_FIELD_T.index(pos), aux)
                    if j == POS_POOLED and not is_start(group, t):
                        pool_columns(group, t - 1)
                    if t == STEP_CROSS3 and j in CROSS3_BANKS:
                        n = CROSS3_BANKS.index(j) * cross3_step
                        cross3(group, range(FIELDS)[n:n + cross3_step])
                    if t == STEP_TOWER and 1 <= j <= MLP1 // P:
                        tower1(group, j - 1)
                    if t == STEP_TOWER and j == 8:
                        tower2(group)
                    if t == STEP_TOWER + 1 and j == 3:
                        tower3(group)

            run(step, pe, before)
            last = GROUPS - 1
            pool_columns(last, GROUP_TILES - 1)
            cross3(last, range(FIELDS))
            for j in range(MLP1 // P):
                tower1(last, j)
            tower2(last)
            tower3(last)

        @block.scalar
        def _(act):
            def double_rows(group):
                act.wait_ge(rows_loaded, at(group, 16 * FIELDS, 16 * FIELDS))
                nc.scalar.activation(rows[:, FIELDS:2 * FIELDS, :], rows[:, 0:FIELDS, :],
                                     ACT.Copy).then_inc(rows_doubled, 1)

            def copy_fields(group, g, bank):
                if g == 0 and not (isinstance(group, int) and group == 0):
                    act.wait_ge(x_field_read, at(group, 1, 0))
                act.wait_ge(field_t_ready, at(group, 4, g + 1))
                nc.scalar.activation(
                    x_field[:, :].rearrange("f (b d) -> f d b", d=EMB)[:, 4 * g:4 * g + 4, :],
                    bank[0:2 * FIELDS, :].rearrange("f (d b) -> f d b", b=P), ACT.Copy).then_inc(field_t_copied, 1)

            def copy_columns(group, c):
                act.wait_ge(tile_t_ready, chunk_count(group, c + 1))
                nc.scalar.activation(x_col[:, c % CHUNKS, :, :],
                                     aux[:, 0:TILES * FIELDS].rearrange("p (i f) -> p i f", f=FIELDS),
                                     ACT.Copy).then_inc(x_col_ready, 1)

            def pair_highs(group, c, k):
                wait_pairs(act, group, c, k)
                if k == 0 and not is_first(group, c):
                    act.wait_ge(cross1_ready, chunk_count(group, c))
                n = block_rows(k)
                nc.scalar.activation(pair_h[0:n, k, :], pairs[0:n, k, :], ACT.Copy).then_inc(pair_high, 1)

            def c1_highs(group, c):
                act.wait_ge(cross1_ready, chunk_count(group, c + 1))
                nc.scalar.activation(c1_h[:, c % 2, :], mid[:, :], ACT.Copy).then_inc(c1_high, 1)

            def save_pooled(group, t):
                act.wait_ge(pool_ready, tile_count(group, t + 1))
                b = SAMPLES * (t % GROUP_TILES)
                nc.scalar.activation(
                    pooled[:, :, b:b + SAMPLES],
                    pool_ps[:, 0:SAMPLES * (FIELDS + 1)].rearrange("g (b f) -> g f b", b=SAMPLES),
                    ACT.Copy).then_inc(pooled_saved, 1)

            def save_out2(group):
                act.wait_ge(pooled_saved, tile_count(group, GROUP_TILES))
                nc.scalar.activation(out2[:, :], pooled[:, FIELDS, :], ACT.Copy).then_inc(out2_ready, 1)

            def before():
                act.wait_ge(consts_ready, 1)
                nc.scalar.activation(warm[:, :], ident[:, 0:1], ACT.Copy)
                double_rows(0)
                for g in range(4):
                    copy_fields(0, g, prod[:, g, :])
                copy_columns(0, 0)
                for k in range(PAIR_BLOCKS):
                    pair_highs(0, 0, k)
                c1_highs(0, 0)
                act.wait_ge(w0_ready, 1)

            def step(group, t):
                c, i = t // TILES, t % TILES
                for j in range(BANKS):
                    if j in ACT_BANKS:
                        if i == 0 and j == 0:
                            act.wait_ge(x_col_ready, chunk_count(group, c + 1))
                        if j == 0 and not (isinstance(group, int) and group == 0 and t < 2):
                            act.wait_ge(c2_ready, tile_count(group, t - 1, 2))
                        act.wait_ge(prod_ready, tile_count(group, t, BANKS) + (j + 1))
                        for f in bank_fields(j):
                            b = f % BANK_FIELDS
                            a = nc.scalar.activation(
                                terms[:, t % 2, ACT_SLOT[f], :],
                                prod[:, (BANKS * t + j) % RING, b * MAPS:(b + 1) * MAPS], ACT.Copy,
                                scale=x_col[:, c % CHUNKS, i, f:f + 1])
                        a.then_inc(act_bank_done, 1)
                    pos = BANKS * i + j
                    if not (is_last(group) and c + 1 >= CHUNKS):
                        if pos in POS_HIGH:
                            pair_highs(group, c + 1, POS_HIGH[pos])
                        if pos == POS_C1_HIGH:
                            c1_highs(group, c + 1)
                        if pos - 2 == POS_TILE_T:
                            copy_columns(group, c + 1)
                    if c % CHUNKS == 2 and pos == POS_ROWS and not is_last(group):
                        double_rows(group + 1)
                    if c % CHUNKS == 2 and pos - 1 in POS_FIELD_T and not is_last(group):
                        copy_fields(group + 1, POS_FIELD_T.index(pos - 1), aux)
                    if j == 1 and not (isinstance(group, int) and group == 0 and t < 2):
                        save_pooled(group, t - 2)
                    if t == GROUP_TILES + 1 and j == 2:
                        save_out2(group)

            run(step, act, before)
            save_pooled(GROUPS - 1, GROUP_TILES - 2)
            save_pooled(GROUPS - 1, GROUP_TILES - 1)
            save_out2(GROUPS - 1)

        @block.vector
        def _(dve):
            def pair_lows(group, c, k):
                first = is_first(group, c)
                wait_pairs(dve, group, c, k)
                dve.wait_ge(pair_high, chunk_count(group, c, PAIR_BLOCKS) + (k + 1))
                if k == 0 and not first:
                    dve.wait_ge(cross1_ready, chunk_count(group, c))
                make_pair_low(nc.vector, k, first_pairs_low if first else dve_pair_low)

            def c1_lows(group, c):
                dve.wait_ge(c1_high, chunk_count(group, c + 1))
                nc.vector.tensor_tensor(c1_l[:, c % 2, :], mid[:, :], c1_h[:, c % 2, :].bitcast(F32),
                                        ALU.subtract).then_inc(c1_low, 1)
                q = c % CHUNKS
                if q == 0 and c > 0:
                    keep_out1(group)
                    dve.wait_ge(out1_ready, at(group, 1, 1))
                nc.vector.tensor_reduce(out1[:, q * CHUNK_SAMPLES:(q + 1) * CHUNK_SAMPLES],
                                        mid[:, :].rearrange("m (b d) -> m b d", d=EMB), AX_X,
                                        ALU.add).then_inc(out1_saved, 1)

            def keep_out1(group):
                dve.wait_ge(out1_saved, chunk_count(group, CHUNKS))
                nc.vector.tensor_copy(out1_done[:, :], out1[:, :]).then_inc(out1_ready, 1)

            def sum_terms(group, t, half):
                dve.wait_ge(act_bank_done, act_count(group, t + 1, 0))
                dve.wait_ge(dve_unit_done, dve_count(group, t + 1, 0))
                if not (isinstance(group, int) and group == 0 and t < 2):
                    dve.wait_ge(pool_ready, tile_count(group, t - 1))
                cols = slice(half * MAPS // 2, (half + 1) * MAPS // 2)
                nc.vector.tensor_reduce(c2[:, t % 2, cols],
                                        terms[:, t % 2, :, cols].rearrange("p s m -> p m s"), AX_X,
                                        ALU.add).then_inc(c2_ready, 1)

            def save_out3(group):
                dve.wait_ge(cross3_ready, at(group, 1, 1))
                nc.vector.tensor_copy(out3[:, :], aux[:, 0:P]).then_inc(out3_ready, 1)

            def relu(ready, saved, dst, bias, n, group):
                dve.wait_ge(ready, at(group, 1, 1))
                for j in range(n):
                    v = nc.vector.tensor_scalar(dst[:, j, :], aux[:, j * P:(j + 1) * P], bias[:, j:j + 1], 0.0,
                                                ALU.add, ALU.max)
                v.then_inc(saved, 1)

            def save_y(group):
                dve.wait_ge(y_ready, at(group, 1, 1))
                nc.vector.tensor_scalar(y_sb[:, bass.ds(group * P, P)], aux[0:1, 0:P], 1.0, None,
                                        ALU.mult).then_inc(y_saved, 1)

            def before():
                nc.vector.memset(w0_b_raw[:, PAIR_BLOCKS - 1, :], 0.0).then_inc(w0_zeroed, 1)
                full = PAIR_BLOCKS - 1
                dve.wait_ge(w0_zeroed, 1)
                dve.wait_ge(w0_loaded, 16 * 4)
                parts = ((slice(0, BLOCK), slice(0, full)),
                         (slice(0, block_rows(full)), slice(full, PAIR_BLOCKS)))
                for r, k in parts:
                    nc.vector.tensor_tensor(w0_sum[r, k, :], w0_a_raw[r, k, :], w0_b_raw[r, k, :],
                                            ALU.add).then_inc(w0_summed, 1)
                dve.wait_ge(w0_summed, 2)
                for r, k in parts:
                    nc.vector.tensor_copy(w0_h[r, k, :], w0_sum[r, k, :]).then_inc(w0_high, 1)
                dve.wait_ge(w0_high, 2)
                for r, k in parts:
                    v = nc.vector.tensor_tensor(w0_l[r, k, :], w0_sum[r, k, :], w0_h[r, k, :].bitcast(F32),
                                                ALU.subtract)
                v.then_inc(w0_ready, 1)
                dve.wait_ge(w1_loaded, 16)
                nc.vector.tensor_copy(w1_h[:, :], w1_raw).then_inc(w1_high, 1)
                dve.wait_ge(w1_high, 1)
                nc.vector.tensor_tensor(w1_l[:, :], w1_raw, w1_h[:, :].bitcast(F32),
                                        ALU.subtract).then_inc(w1_ready, 1)
                dve.wait_ge(one_loaded, 16 * BLOCK_SHIFTS)
                for k in range(PAIR_BLOCKS + 1):
                    if k < PAIR_BLOCKS:
                        dve.wait_ge(other_loaded[k], 16 * len(block_shifts(k)))
                        make_pairs(nc.vector, k, first_pairs_ready)
                    if k > 0:
                        pair_lows(0, 0, k - 1)
                c1_lows(0, 0)

            def step(group, t):
                c, i = t // TILES, t % TILES
                for j in range(BANKS):
                    if j in DVE_BANKS:
                        if j == DVE_BANKS[0]:
                            dve.wait_ge(x_col_ready, chunk_count(group, c + 1))
                        dve.wait_ge(prod_ready, tile_count(group, t, BANKS) + (j + 1))
                        for f in bank_fields(j):
                            b, n = f % BANK_FIELDS, DVE_ORDER.index(f)
                            src = prod[:, (BANKS * t + j) % RING, b * MAPS:(b + 1) * MAPS]
                            x = x_col[:, c % CHUNKS, i, f:f + 1]
                            acc = terms[:, t % 2, SLOTS - 2 + n % 2, :]
                            if n < 2:
                                v = nc.vector.tensor_scalar(acc, src, x, None, ALU.mult)
                            else:
                                dve.wait_ge(dve_unit_done, dve_count(group, t, n - 1))
                                v = nc.vector.scalar_tensor_tensor(out=acc, in0=src, scalar=x, in1=acc,
                                                                   op0=ALU.mult, op1=ALU.add)
                            v.then_inc(dve_unit_done, 1)
                    if j == 1 and not is_start(group, t):
                        sum_terms(group, t - 1, 0)
                    if j == 5 and not is_start(group, t):
                        sum_terms(group, t - 1, 1)
                    pos = BANKS * i + j
                    if not (is_last(group) and c + 1 >= CHUNKS):
                        if pos in POS_LOW and not pool_makes_low(c + 1):
                            pair_lows(group, c + 1, POS_LOW[pos])
                        if pos == POS_C1_LOW:
                            c1_lows(group, c + 1)
                    if t == STEP_CROSS3 and j == 9:
                        save_out3(group)
                    if t == STEP_TOWER and j == 6:
                        relu(h1_ready, h1_saved, h1, bt1_sb, MLP1 // P, group)
                    if t == STEP_TOWER + 1 and j == 0:
                        relu(h2_ready, h2_saved, h2, bt2_sb, MLP2 // P, group)
                    if t == STEP_TOWER + 1 and j == 5:
                        save_y(group)

            run(step, dve, before)
            last = GROUPS - 1
            sum_terms(last, GROUP_TILES - 1, 0)
            sum_terms(last, GROUP_TILES - 1, 1)
            keep_out1(last)
            save_out3(last)
            relu(h1_ready, h1_saved, h1, bt1_sb, MLP1 // P, last)
            relu(h2_ready, h2_saved, h2, bt2_sb, MLP2 // P, last)
            save_y(last)


def kernel(**inputs):
    import concourse.bacc as bacc
    from concourse.bass_utils import run_bass_kernel_spmd

    f = np.tile(np.arange(FIELDS), SHIFTS)
    g = (f + SHIFT0 + np.repeat(np.arange(SHIFTS), FIELDS)) % FIELDS
    w0 = np.asarray(inputs["L0_rec_f0"])
    arrays = {
        "ids": np.asarray(inputs["ids"]),
        "dense_t": np.asarray(inputs["dense_ctx"]).T,
        "w0_a": w0[f * FIELDS + g],
        "w0_b": w0[(g * FIELDS + f)[:CROSS]],
        "w1": inputs["L0_rec_f1"],
        "w2": inputs["L0_rec_f2"],
        "wt1": inputs["W_top1"],
        "bt1": np.asarray(inputs["b_top1"]).reshape(MLP1 // P, P).T,
        "wt2": inputs["W_top2"],
        "bt2": np.asarray(inputs["b_top2"]).reshape(MLP2 // P, P).T,
        "wt3": np.asarray(inputs["W_top3"]).reshape(MLP2 // P, P).T,
    }
    for n in range(FIELDS):
        arrays[f"tbl_{n}"] = inputs[f"tbl_{n}"]
    arrays = {n: np.ascontiguousarray(a) for n, a in arrays.items()}

    nc = bacc.Bacc("TRN2", target_bir_lowering=False, num_devices=1)
    ap = {n: nc.dram_tensor(n, a.shape, mybir.dt.from_np(a.dtype), kind="ExternalInput").ap()
          for n, a in arrays.items()}
    out = nc.dram_tensor("y", (1, BATCH), F32, kind="ExternalOutput").ap()
    cin_program(nc, ap["ids"], [ap[f"tbl_{n}"] for n in range(FIELDS)], ap["dense_t"], ap["w0_a"], ap["w0_b"],
                ap["w1"], ap["w2"], ap["wt1"], ap["bt1"], ap["wt2"], ap["bt2"], ap["wt3"], out)
    result = run_bass_kernel_spmd(nc, [arrays], core_ids=[0])
    return result.results[0]["y"].reshape(BATCH, 1)
```

```python
from contextlib import ExitStack

import numpy as np

import concourse.bass as bass
from concourse import mybir
from concourse.alu_op_type import AluOpType as ALU

F32 = mybir.dt.float32
F32R = mybir.dt.float32r
I32 = mybir.dt.int32
ACT = mybir.ActivationFunctionType
AX_X = mybir.AxisListType.X

FIELDS = 39
EMB = 16
BATCH = 512
MAPS = 128
P = 128

SAMPLES = P // EMB
TILES = 4
CHUNKS = 4
GROUPS = BATCH // P
GROUP_TILES = TILES * CHUNKS
CHUNK = TILES * P
CHUNK_SAMPLES = TILES * SAMPLES

SHIFTS = (FIELDS + 1) // 2
SHIFT0 = FIELDS - SHIFTS + 1
PAIRS = SHIFTS * FIELDS
CROSS = PAIRS - FIELDS
BLOCK_SHIFTS = P // FIELDS
BLOCK = BLOCK_SHIFTS * FIELDS
PAIR_BLOCKS = -(-SHIFTS // BLOCK_SHIFTS)


def block_shifts(k):
    return range(BLOCK_SHIFTS * k, min(BLOCK_SHIFTS * (k + 1), SHIFTS))


def block_rows(k):
    return len(block_shifts(k)) * FIELDS


BANK_FIELDS = 4
BANKS = -(-FIELDS // BANK_FIELDS)
RING = 5
ACT_BANKS = (0, 2, 3, 5, 6, 8, 9)
DVE_BANKS = (1, 4, 7)
assert sorted(ACT_BANKS + DVE_BANKS) == list(range(BANKS))


def bank_fields(j):
    return range(BANK_FIELDS * j, min(BANK_FIELDS * (j + 1), FIELDS))


ACT_SLOT = {f: n for n, f in enumerate(f for j in ACT_BANKS for f in bank_fields(j))}
DVE_ORDER = [f for j in DVE_BANKS for f in bank_fields(j)]
SLOTS = len(ACT_SLOT) + 2

PE_SPREAD = 3

POS_CROSS1 = (0, 6, 11, 16, 21, 26, 31)
POS_CROSS1_LATE = (9, 13, 17, 20, 24, 28, 31)
POS_C1_HIGH = 33
POS_C1_LOW = 35
POS_TILE_T = 5
POS_ROWS = 22
POS_FIELD_T = (24, 28, 32, 36)
SUM_BANKS = (1, 3, 5, 8)
SUM_PARTS = len(SUM_BANKS)
POS_POOLED = 3
POS_CROSS3 = (177, 178, 179, 180, 181, 182)
POS_OUT2 = 181
POS_OUT3 = 183
POS_TOWER1 = (185, 186, 187, 188)
POS_RELU1 = 189
POS_TOWER2 = 191
POS_RELU2 = 192
POS_TOWER3 = 196
POS_Y = 197
FIRST = 4
WARM_UP = 26
KEEP_UP = 16
EARLY_ROWS = 32
GATHER_STEPS = 6
DVE_CHUNK = 2
DVE_PAIRS = {12: 4, 16: 5, 22: 6}

MLP1 = 512
MLP2 = 256
DENSE = 16
K_MLP1 = 3


def at(group, per_group, const):
    return group * per_group + const


def cin_program(nc, ids, tables, dense_t, w0_a, w0_b, w1, w2, wt1, bt1, wt2, bt2, wt3, select, out):
    with ExitStack() as ctx:
        def sb(name, shape, dt=F32):
            return ctx.enter_context(nc.sbuf_tensor(name, shape, dt))

        def sem(name):
            return ctx.enter_context(nc.semaphore(name))

        prod = ctx.enter_context(nc.psum_tensor("prod", [P, RING, 512], F32))
        aux = ctx.enter_context(nc.psum_tensor("aux", [P, 512], F32))
        mid = ctx.enter_context(nc.psum_tensor("mid", [P, 512], F32))
        pool_ps = ctx.enter_context(nc.psum_tensor("pool_ps", [P, 512], F32))

        ids_sb = sb("ids_sb", [P, FIELDS], I32)
        rows = sb("rows", [P, 2 * FIELDS, EMB])
        x_field = sb("x_field", [2 * FIELDS, P * EMB])
        x_col = sb("x_col", [P, CHUNKS, TILES, FIELDS])
        pair_one = sb("pair_one", [BLOCK, 2, CHUNK])
        pairs = sb("pairs", [BLOCK, 2, PAIR_BLOCKS, CHUNK])
        w0_sum = sb("w0_sum", [BLOCK, PAIR_BLOCKS, MAPS])
        w1_h = sb("w1_h", [P, FIELDS * MAPS], F32R)
        w1_l = sb("w1_l", [P, FIELDS * MAPS], F32R)
        w2_sb = sb("w2_sb", [P, FIELDS * MAPS])
        c1_h = sb("c1_h", [P, 2, CHUNK], F32R)
        c1_l = sb("c1_l", [P, 2, CHUNK], F32R)
        terms = sb("terms", [P, 2, SLOTS, MAPS])
        c2 = sb("c2", [P, 2, MAPS])
        x_diag = sb("x_diag", [P, TILES, SAMPLES, FIELDS + 1])
        pooled = sb("pooled", [P, FIELDS + 1, P])
        out1 = sb("out1", [P, P])
        out1_done = sb("out1_done", [P, P])
        out2 = sb("out2", [P, P])
        out3 = sb("out3", [P, P])
        dense_sb = sb("dense_sb", [DENSE, BATCH])
        wt1_sb = sb("wt1_sb", [P, K_MLP1, MLP1])
        wt1_d = sb("wt1_d", [DENSE, MLP1])
        wt2_sb = sb("wt2_sb", [P, MLP1 // P, MLP2])
        wt3_sb = sb("wt3_sb", [P, MLP2 // P])
        bt1_sb = sb("bt1_sb", [P, MLP1 // P])
        bt2_sb = sb("bt2_sb", [P, MLP2 // P])
        h1 = sb("h1", [P, MLP1 // P, P])
        h2 = sb("h2", [P, MLP2 // P, P])
        y_sb = sb("y_sb", [1, BATCH])
        ident = sb("ident", [P, P])
        select_sb = sb("select_sb", [FIELDS, PE_SPREAD + 1, BLOCK])
        own = sb("own", [P, SAMPLES])
        warm = sb("warm", [P, 1])

        w1_raw = pooled[:, :, :].rearrange("p f b -> p (f b)")[:, 0:FIELDS * MAPS]
        w0_a_raw = terms[:, 0, 0:PAIR_BLOCKS, :]
        w0_b_raw = terms[:, 0, PAIR_BLOCKS:2 * PAIR_BLOCKS, :]

        ids_loaded = sem("ids_loaded")
        w0_loaded = sem("w0_loaded")
        w1_loaded = sem("w1_loaded")
        w2_loaded = sem("w2_loaded")
        tower_loaded = sem("tower_loaded")
        select_loaded = sem("select_loaded")
        early_rows_loaded = sem("early_rows_loaded")
        rows_loaded = sem("rows_loaded")
        rows_doubled = sem("rows_doubled")
        consts_step = sem("consts_step")
        consts_ready = sem("consts_ready")
        w0_zeroed = sem("w0_zeroed")
        w0_ready = sem("w0_ready")
        w1_high = sem("w1_high")
        w1_ready = sem("w1_ready")
        field_t_ready = sem("field_t_ready")
        field_t_copied = sem("field_t_copied")
        tile_t_ready = sem("tile_t_ready")
        x_col_ready = sem("x_col_ready")
        one_loaded = [sem(f"one_loaded_{n}") for n in range(2)]
        other_loaded = [[sem(f"other_loaded_{n}_{k}") for k in range(PAIR_BLOCKS)] for n in range(2)]
        pe_spread = sem("pe_spread")
        one_copied = sem("one_copied")
        first_pairs_ready = sem("first_pairs_ready")
        dve_pairs_ready = sem("dve_pairs_ready")
        pairs_ready = sem("pairs_ready")
        cross1_ready = sem("cross1_ready")
        c1_high = sem("c1_high")
        c1_low = sem("c1_low")
        out1_saved = sem("out1_saved")
        out1_ready = sem("out1_ready")
        prod_ready = sem("prod_ready")
        act_bank_done = sem("act_bank_done")
        dve_unit_done = sem("dve_unit_done")
        c2_ready = sem("c2_ready")
        x_diag_ready = sem("x_diag_ready")
        pool_ready = sem("pool_ready")
        pooled_saved = sem("pooled_saved")
        cross3_ready = sem("cross3_ready")
        out2_ready = sem("out2_ready")
        out3_ready = sem("out3_ready")
        h1_ready = sem("h1_ready")
        h1_saved = sem("h1_saved")
        h2_ready = sem("h2_ready")
        h2_saved = sem("h2_saved")
        y_ready = sem("y_ready")
        y_saved = sem("y_saved")
        y_stored = sem("y_stored")

        def act_count(group, t, n):
            return at(group, len(ACT_BANKS) * GROUP_TILES, len(ACT_BANKS) * t + n)

        def dve_count(group, t, n):
            return at(group, len(DVE_ORDER) * GROUP_TILES, len(DVE_ORDER) * t + n)

        def tile_count(group, t, per_tile=1):
            return at(group, per_tile * GROUP_TILES, per_tile * t)

        def rows_count(group):
            return at(group, 16 * FIELDS, 16 * (FIELDS - EARLY_ROWS))

        def chunk_count(group, c, per_chunk=1):
            return at(group, per_chunk * CHUNKS, per_chunk * c)

        def parity_count(group, c, per_chunk, by_pe=False):
            return at(group, per_chunk * CHUNKS // 2, per_chunk * (c // 2 + 1 - (by_pe and c % 2 == 0)))

        def is_first(group, c):
            return isinstance(group, int) and group == 0 and c == 0

        def wait_pairs(eng, group, c, k):
            if is_first(group, c):
                eng.wait_ge(first_pairs_ready, k + 1)
            else:
                groups, q = c // CHUNKS, c % CHUNKS
                by_dve = list(DVE_PAIRS.values())
                if q == DVE_CHUNK and k in by_dve:
                    eng.wait_ge(dve_pairs_ready, at(group, len(by_dve), groups * len(by_dve) + by_dve.index(k) + 1))
                else:
                    per_group = CHUNKS * PAIR_BLOCKS - len(by_dve)
                    done = groups * per_group + q * PAIR_BLOCKS - (len(by_dve) if q > DVE_CHUNK else 0) + k + 1
                    eng.wait_ge(pairs_ready, at(group, per_group, done - PAIR_BLOCKS))

        def make_pairs(ns, c, k, done):
            n = block_rows(k)
            ns.tensor_tensor(pairs[0:n, c % 2, k, :], pairs[0:n, c % 2, k, :], pair_one[0:n, c % 2, :],
                             ALU.mult).then_inc(done, 1)

        def comes_late(group, c):
            return c % CHUNKS == 0 or isinstance(group, int) and group == 0 and c == 1

        def pool_products(group, c, i):
            todo = [(c + 1, k) for k in ((1,), (2, 3), (4, 5, 6), ())[i]]
            if i == 0 and comes_late(group, c + 1):
                todo = [(c + 1, 0)] + todo
            if i == TILES - 1 and not comes_late(group, c + 2):
                todo = todo + [(c + 2, 0)]
            return [(chunk, k) for chunk, k in todo if not (is_last(group) and chunk >= CHUNKS)
                    and not (chunk % CHUNKS == DVE_CHUNK and k in DVE_PAIRS.values())]

        def wait_spread(eng, group, c, k):
            eng.wait_ge(one_loaded[c % 2], parity_count(group, c, 16 * BLOCK_SHIFTS, by_pe=True))
            eng.wait_ge(other_loaded[c % 2][k],
                        parity_count(group, c, 16 * len(block_shifts(k)), by_pe=k < PE_SPREAD))

        def run(step, eng, before):
            before()
            for t in range(FIRST):
                step(0, t)
            with eng.Fori(0, GROUPS - 1) as group:
                for t in range(FIRST, FIRST + GROUP_TILES):
                    step(group, t)
            for t in range(FIRST, GROUP_TILES):
                step(GROUPS - 1, t)

        def is_last(group):
            return isinstance(group, int) and group == GROUPS - 1

        def is_start(group, t):
            return isinstance(group, int) and group == 0 and t == 0

        block = ctx.enter_context(nc.Block())

        @block.sync
        def _(sp):
            sp.dma_start(ids_sb[:, :], ids[0:P, :]).then_inc(ids_loaded, 16)
            sp.dma_start(select_sb[:, :, :], select).then_inc(select_loaded, 16)
            full, rest = (PAIR_BLOCKS - 1) * BLOCK, block_rows(PAIR_BLOCKS - 1)
            sp.dma_start(w0_a_raw[0:BLOCK, 0:PAIR_BLOCKS - 1, :],
                         w0_a[0:full, :].rearrange("(k p) m -> p k m", p=BLOCK)).then_inc(w0_loaded, 16)
            sp.dma_start(w0_a_raw[0:rest, PAIR_BLOCKS - 1, :], w0_a[full:PAIRS, :]).then_inc(w0_loaded, 16)
            sp.dma_start(w0_b_raw[0:BLOCK, 0:PAIR_BLOCKS - 1, :],
                         w0_b[0:full, :].rearrange("(k p) m -> p k m", p=BLOCK)).then_inc(w0_loaded, 16)
            sp.wait_ge(w0_zeroed, 1)
            sp.dma_start(w0_b_raw[0:CROSS - full, PAIR_BLOCKS - 1, :], w0_b[full:CROSS, :]).then_inc(w0_loaded, 16)
            sp.dma_start(w1_raw.rearrange("g (f m) -> g f m", m=MAPS),
                         w1.rearrange("(f g) m -> g f m", g=MAPS)).then_inc(w1_loaded, 16)
            sp.dma_start(w2_sb[:, :].rearrange("g (f m) -> g f m", m=MAPS),
                         w2.rearrange("(f g) m -> g f m", g=MAPS)).then_inc(w2_loaded, 16)
            sp.dma_start(wt1_sb[:, :, :], wt1[0:K_MLP1 * P, :].rearrange("(k p) m -> p k m", p=P)).then_inc(tower_loaded, 16)
            sp.dma_start(wt1_d[:, :], wt1[K_MLP1 * P:, :]).then_inc(tower_loaded, 16)
            sp.dma_start(wt2_sb[:, :, :], wt2.rearrange("(k p) m -> p k m", p=P)).then_inc(tower_loaded, 16)
            sp.dma_start(wt3_sb[:, :], wt3).then_inc(tower_loaded, 16)
            sp.dma_start(bt1_sb[:, :], bt1).then_inc(tower_loaded, 16)
            sp.dma_start(bt2_sb[:, :], bt2).then_inc(tower_loaded, 16)
            sp.dma_start(dense_sb[:, :], dense_t).then_inc(tower_loaded, 16)

            def spread_fields(group, c, blocks=range(PAIR_BLOCKS)):
                cols = slice((c % CHUNKS) * CHUNK, (c % CHUNKS + 1) * CHUNK)
                if c % CHUNKS == 0:
                    sp.wait_ge(field_t_copied, at(group, len(POS_FIELD_T), (c // CHUNKS + 1) * len(POS_FIELD_T)))
                elif not (isinstance(group, int) and group == 0 and c < 2):
                    sp.wait_ge(cross1_ready, chunk_count(group, c - 1))
                for r in range(BLOCK_SHIFTS) if 0 in blocks else ():
                    sp.dma_start(pair_one[r * FIELDS:(r + 1) * FIELDS, c % 2, :],
                                 x_field[0:FIELDS, cols]).then_inc(one_loaded[c % 2], 16)
                for k in blocks:
                    for r, t in enumerate(block_shifts(k)):
                        sp.dma_start(pairs[r * FIELDS:(r + 1) * FIELDS, c % 2, k, :],
                                     x_field[SHIFT0 + t:SHIFT0 + t + FIELDS, cols]).then_inc(other_loaded[c % 2][k], 16)

            spread_fields(0, 0, range(PE_SPREAD, PAIR_BLOCKS))
            spread_fields(0, 1)
            sp.wait_ge(early_rows_loaded, 16 * EARLY_ROWS)
            with sp.Fori(0, GROUPS - 1) as group:
                sp.wait_ge(rows_loaded, rows_count(group))
                sp.dma_start(ids_sb[:, :], ids[bass.ds(group * P + P, P), :]).then_inc(ids_loaded, 16)
                for c in range(2, 2 + CHUNKS):
                    spread_fields(group, c)
            for c in range(2, CHUNKS):
                spread_fields(GROUPS - 1, c)
            sp.wait_ge(y_saved, GROUPS)
            sp.dma_start(out, y_sb[:, :]).then_inc(y_stored, 16)
            sp.wait_ge(y_stored, 16)

        @block.gpsimd
        def _(pool):
            def gather(fields, done=rows_loaded):
                for f in fields:
                    nc.gpsimd.indirect_dma_start(
                        rows[:, f, :], None, tables[f],
                        bass.IndirectOffsetOnAxis(ap=ids_sb[:, f:f + 1], axis=0)).then_inc(done, 16)

            def products(group, c, k):
                wait_spread(pool, group, c, k)
                make_pairs(nc.gpsimd, c, k, pairs_ready)

            def before():
                nc.gpsimd.memset(ident[:, :], 0.0).then_inc(consts_step, 1)
                nc.gpsimd.memset(own[:, :], 1.0).then_inc(consts_step, 1)
                pool.wait_ge(consts_step, 2)
                nc.gpsimd.affine_select(out=ident[:, :], in_=ident[:, :], compare_op=ALU.not_equal, fill=1.0,
                                        base=0, pattern=[[-1, P]], channel_multiplier=1)
                nc.gpsimd.affine_select(out=own[:, :], in_=own[:, :], compare_op=ALU.is_ge, fill=0.0,
                                        base=0, pattern=[[-EMB, SAMPLES]], channel_multiplier=1).then_inc(consts_step, 1)
                pool.wait_ge(consts_step, 3)
                nc.gpsimd.affine_select(out=own[:, :], in_=own[:, :], compare_op=ALU.is_ge, fill=0.0,
                                        base=EMB - 1, pattern=[[EMB, SAMPLES]], channel_multiplier=-1).then_inc(consts_step, 1)
                pool.wait_ge(consts_step, 4)
                nc.gpsimd.tensor_copy(x_diag[:, :, :, FIELDS],
                                      own[:, :].unsqueeze(1).broadcast_to([P, TILES, SAMPLES])).then_inc(consts_ready, 1)
                pool.wait_ge(ids_loaded, 16)
                gather(range(EARLY_ROWS), early_rows_loaded)
                gather(range(EARLY_ROWS, FIELDS))

            per_step = -(-FIELDS // GATHER_STEPS)

            def step(group, t):
                c, i = t // TILES, t % TILES
                gathers = FIRST <= t < FIRST + GATHER_STEPS and not is_last(group)
                if gathers and t == FIRST:
                    pool.wait_ge(ids_loaded, at(group, 16, 32))
                    pool.wait_ge(field_t_ready, at(group, len(POS_FIELD_T), len(POS_FIELD_T)))
                pool.wait_ge(x_col_ready, chunk_count(group, c + 1))
                if not (isinstance(group, int) and group == 0 and t < TILES):
                    pool.wait_ge(pool_ready, tile_count(group, t - TILES + 1))
                nc.gpsimd.tensor_tensor(
                    x_diag[:, i, :, 0:FIELDS],
                    x_col[:, c % CHUNKS, i, 0:FIELDS].unsqueeze(1).broadcast_to([P, SAMPLES, FIELDS]),
                    own[:, :].unsqueeze(2).broadcast_to([P, SAMPLES, FIELDS]), ALU.mult).then_inc(x_diag_ready, 1)
                for chunk, k in pool_products(group, c, i):
                    products(group, chunk, k)
                if gathers:
                    gather(range(FIELDS)[(t - FIRST) * per_step:(t - FIRST + 1) * per_step])

            run(step, pool, before)

        @block.tensor
        def _(pe):
            def field_transposes(group, g, bank):
                pe.wait_ge(consts_ready, 1)
                if g == 0:
                    pe.wait_ge(rows_doubled, at(group, 1, 2))
                    if not (isinstance(group, int) and group == 0):
                        pe.wait_ge(x_col_ready, chunk_count(group, 0))
                elif bank is aux:
                    pe.wait_ge(field_t_copied, at(group, len(POS_FIELD_T), g))
                for d in range(4):
                    dst, src = bank[0:2 * FIELDS, d * P:(d + 1) * P], rows[:, :, 4 * g + d]
                    if d == 0 and not isinstance(group, int):
                        mm = pe.matmul(dst, src, ident[:, :], start=True, stop=True)
                    else:
                        mm = pe.transpose(dst, src, ident[:, :])
                mm.then_inc(field_t_ready, 1)

            def tile_transposes(group, c):
                pe.wait_ge(consts_ready, 1)
                if c % CHUNKS == 0:
                    pe.wait_ge(field_t_copied, at(group, len(POS_FIELD_T), (c // CHUNKS + 1) * len(POS_FIELD_T)))
                if not is_first(group, c):
                    pe.wait_ge(x_col_ready, chunk_count(group, c))
                for i in range(TILES):
                    cols = (c % CHUNKS * TILES + i) * P
                    dst, src = aux[:, i * FIELDS:(i + 1) * FIELDS], x_field[0:FIELDS, cols:cols + P]
                    if i > 0 or isinstance(group, int):
                        mm = pe.transpose(dst, src, ident[0:FIELDS, 0:FIELDS])
                    else:
                        mm = pe.matmul(dst, src, ident[0:FIELDS, 0:FIELDS], start=True, stop=True)
                mm.then_inc(tile_t_ready, 1)

            def cross1(group, c, k):
                if k == 0:
                    if is_first(group, c):
                        pe.wait_ge(w0_ready, 1)
                    else:
                        pe.wait_ge(out1_saved, chunk_count(group, c))
                wait_pairs(pe, group, c, k)
                n = block_rows(k)
                mm = pe.matmul(mid[:, :], w0_sum[0:n, k, :], pairs[0:n, c % 2, k, :],
                               start=(k == 0), stop=(k == PAIR_BLOCKS - 1))
                if k == PAIR_BLOCKS - 1:
                    mm.then_inc(cross1_ready, 1)

            def pool_columns(group, t):
                pe.wait_ge(c2_ready, tile_count(group, t + 1, SUM_PARTS))
                pe.wait_ge(x_diag_ready, tile_count(group, t + 1))
                if not is_start(group, t):
                    pe.wait_ge(pooled_saved, tile_count(group, t))
                n = SAMPLES * (FIELDS + 1)
                pe.matmul(pool_ps[:, 0:n], c2[:, t % 2, :],
                          x_diag[:, t % TILES, :, :].rearrange("p b f -> p (b f)"),
                          start=True, stop=True).then_inc(pool_ready, 1)

            def cross3(group, fields):
                if fields[0] == 0:
                    pe.wait_ge(pooled_saved, tile_count(group, GROUP_TILES))
                    pe.wait_ge(w2_loaded, 16)
                for f in fields:
                    mm = pe.matmul(aux[:, 0:P], w2_sb[:, f * MAPS:(f + 1) * MAPS], pooled[:, f, :],
                                   start=(f == 0), stop=(f == FIELDS - 1))
                if fields[-1] == FIELDS - 1:
                    mm.then_inc(cross3_ready, 1)

            def tower1(group, j):
                if j == 0:
                    pe.wait_ge(out3_ready, at(group, 1, 1))
                    pe.wait_ge(out1_ready, at(group, 1, 1))
                    pe.wait_ge(out2_ready, at(group, 1, 1))
                    pe.wait_ge(tower_loaded, 16 * 7)
                cols = slice(j * P, (j + 1) * P)
                for k, z in enumerate((out1_done[:, :], out2[:, :], out3[:, :])):
                    pe.matmul(aux[:, cols], wt1_sb[:, k, cols], z, start=(k == 0), stop=False)
                mm = pe.matmul(aux[:, cols], wt1_d[:, cols], dense_sb[:, bass.ds(group * P, P)],
                               start=False, stop=True)
                if j == MLP1 // P - 1:
                    mm.then_inc(h1_ready, 1)

            def tower2(group):
                pe.wait_ge(h1_saved, at(group, 1, 1))
                for j in range(MLP2 // P):
                    cols = slice(j * P, (j + 1) * P)
                    for k in range(MLP1 // P):
                        mm = pe.matmul(aux[:, cols], wt2_sb[:, k, cols], h1[:, k, :],
                                       start=(k == 0), stop=(k == MLP1 // P - 1))
                mm.then_inc(h2_ready, 1)

            def tower3(group):
                pe.wait_ge(h2_saved, at(group, 1, 1))
                for k in range(MLP2 // P):
                    mm = pe.matmul(aux[0:1, 0:P], wt3_sb[:, k:k + 1], h2[:, k, :],
                                   start=(k == 0), stop=(k == MLP2 // P - 1))
                mm.then_inc(y_ready, 1)

            def keep_busy(times):
                for _ in range(times):
                    pe.matmul(mid[:, :], w1_h[:, 0:MAPS], w1_h[:, 0:512], start=True, stop=True)

            def before():
                pe.wait_ge(w1_ready, 1)
                pe.wait_ge(early_rows_loaded, 16 * EARLY_ROWS)
                keep_busy(WARM_UP)
                for g in range(len(POS_FIELD_T)):
                    field_transposes(0, g, prod[:, g, :])
                pe.wait_ge(select_loaded, 16)
                pe.wait_ge(field_t_copied, len(POS_FIELD_T))
                for n in range(PE_SPREAD + 1):
                    pe.matmul(prod[0:BLOCK, n, :], select_sb[:, n, :], x_field[0:FIELDS, 0:CHUNK],
                              start=True, stop=True).then_inc(pe_spread, 1)
                for k in range(PAIR_BLOCKS):
                    cross1(0, 0, k)
                tile_transposes(0, 0)

            cross3_step = -(-FIELDS // len(POS_CROSS3))

            def step(group, t):
                c, i = t // TILES, t % TILES
                for j in range(BANKS):
                    n = BANKS * t + j
                    if i == 0 and j == 0:
                        pe.wait_ge(c1_high, chunk_count(group, c + 1))
                        if is_start(group, t):
                            pe.wait_ge(w1_ready, 1)
                    if not (isinstance(group, int) and group == 0 and n < RING):
                        tb, jb = (n - RING) // BANKS, (n - RING) % BANKS
                        if jb in ACT_BANKS:
                            pe.wait_ge(act_bank_done, act_count(group, tb, ACT_BANKS.index(jb) + 1))
                        else:
                            pe.wait_ge(dve_unit_done, dve_count(group, tb, BANK_FIELDS * (DVE_BANKS.index(jb) + 1)))
                    fs = bank_fields(j)
                    cols = slice(fs[0] * MAPS, (fs[-1] + 1) * MAPS)
                    bank = prod[:, n % RING, 0:len(fs) * MAPS]
                    high = c1_h[:, c % 2, i * P:(i + 1) * P]
                    low = c1_l[:, c % 2, i * P:(i + 1) * P]
                    pe.matmul(bank, high, w1_h[:, cols], start=True, stop=False)
                    pe.matmul(bank, high, w1_l[:, cols], start=False, stop=False)
                    if i == 0 and j == 0:
                        pe.wait_ge(c1_low, chunk_count(group, c + 1))
                    pe.matmul(bank, low, w1_h[:, cols], start=False, stop=True).then_inc(prod_ready, 1)

                    pos = BANKS * i + j
                    next_chunk = not (is_last(group) and c + 1 >= CHUNKS)
                    if next_chunk:
                        positions = POS_CROSS1_LATE if comes_late(group, c + 1) else POS_CROSS1
                        if pos in positions:
                            cross1(group, c + 1, positions.index(pos))
                        if pos == POS_TILE_T:
                            tile_transposes(group, c + 1)
                    if c % CHUNKS == 2 and pos in POS_FIELD_T and not is_last(group):
                        field_transposes(group + 1, POS_FIELD_T.index(pos), aux)
                    if j == POS_POOLED and not (isinstance(group, int) and group == 0 and t < 2):
                        pool_columns(group, t - 2)
                    if n in POS_CROSS3:
                        first = POS_CROSS3.index(n) * cross3_step
                        cross3(group, range(FIELDS)[first:first + cross3_step])
                    if n in POS_TOWER1:
                        tower1(group, POS_TOWER1.index(n))
                    if n == POS_TOWER2:
                        tower2(group)
                    if n == POS_TOWER3:
                        tower3(group)

            run(step, pe, before)
            last = GROUPS - 1
            pool_columns(last, GROUP_TILES - 2)
            keep_busy(KEEP_UP)
            pool_columns(last, GROUP_TILES - 1)
            cross3(last, range(FIELDS))
            for j in range(MLP1 // P):
                tower1(last, j)
            tower2(last)
            tower3(last)

        @block.scalar
        def _(act):
            def copy_fields(group, g, bank):
                if g == 0 and not (isinstance(group, int) and group == 0):
                    wait_pairs(act, group, -1, PAIR_BLOCKS - 1)
                act.wait_ge(field_t_ready, at(group, len(POS_FIELD_T), g + 1))
                nc.scalar.activation(
                    x_field[:, :].rearrange("f (b d) -> f d b", d=EMB)[:, 4 * g:4 * g + 4, :],
                    bank[0:2 * FIELDS, :].rearrange("f (d b) -> f d b", b=P), ACT.Copy).then_inc(field_t_copied, 1)

            def copy_columns(group, c):
                act.wait_ge(tile_t_ready, chunk_count(group, c + 1))
                nc.scalar.activation(x_col[:, c % CHUNKS, :, :],
                                     aux[:, 0:TILES * FIELDS].rearrange("p (i f) -> p i f", f=FIELDS),
                                     ACT.Copy).then_inc(x_col_ready, 1)

            def c1_highs(group, c):
                act.wait_ge(cross1_ready, chunk_count(group, c + 1))
                nc.scalar.activation(c1_h[:, c % 2, :], mid[:, :], ACT.Copy).then_inc(c1_high, 1)

            def save_pooled(group, t):
                act.wait_ge(pool_ready, tile_count(group, t + 1))
                if t == GROUP_TILES:
                    act.wait_ge(out2_ready, at(group, 1, 1))
                b = SAMPLES * (t % GROUP_TILES)
                nc.scalar.activation(
                    pooled[:, :, b:b + SAMPLES],
                    pool_ps[:, 0:SAMPLES * (FIELDS + 1)].rearrange("g (b f) -> g f b", b=SAMPLES),
                    ACT.Copy).then_inc(pooled_saved, 1)

            def save_out2(group):
                act.wait_ge(pooled_saved, tile_count(group, GROUP_TILES))
                nc.scalar.activation(out2[:, :], pooled[:, FIELDS, :], ACT.Copy).then_inc(out2_ready, 1)

            def before():
                act.wait_ge(consts_ready, 1)
                nc.scalar.activation(warm[:, :], ident[:, 0:1], ACT.Copy)
                for g in range(len(POS_FIELD_T)):
                    copy_fields(0, g, prod[:, g, :])
                act.wait_ge(pe_spread, 1)
                nc.scalar.activation(pair_one[:, 0, :], prod[0:BLOCK, 0, :], ACT.Copy).then_inc(one_copied, 1)
                c1_highs(0, 0)
                copy_columns(0, 0)
                act.wait_ge(w0_ready, 1)

            def step(group, t):
                c, i = t // TILES, t % TILES
                for j in range(BANKS):
                    if j in ACT_BANKS:
                        if i == 0 and j == 0:
                            act.wait_ge(x_col_ready, chunk_count(group, c + 1))
                        if j == 0 and not (isinstance(group, int) and group == 0 and t < 2):
                            act.wait_ge(c2_ready, tile_count(group, t - 1, SUM_PARTS))
                        act.wait_ge(prod_ready, tile_count(group, t, BANKS) + (j + 1))
                        for f in bank_fields(j):
                            b = f % BANK_FIELDS
                            a = nc.scalar.activation(
                                terms[:, t % 2, ACT_SLOT[f], :],
                                prod[:, (BANKS * t + j) % RING, b * MAPS:(b + 1) * MAPS], ACT.Copy,
                                scale=x_col[:, c % CHUNKS, i, f:f + 1])
                        a.then_inc(act_bank_done, 1)
                    pos = BANKS * i + j
                    if not (is_last(group) and c + 1 >= CHUNKS):
                        if pos == POS_C1_HIGH:
                            c1_highs(group, c + 1)
                        if pos - 2 == POS_TILE_T:
                            copy_columns(group, c + 1)
                    if c % CHUNKS == 2 and pos - 1 in POS_FIELD_T and not is_last(group):
                        copy_fields(group + 1, POS_FIELD_T.index(pos - 1), aux)
                    if j == POS_POOLED + 2 and not (isinstance(group, int) and group == 0 and t < 2):
                        save_pooled(group, t - 2)
                    if BANKS * t + j == POS_OUT2:
                        save_out2(group)

            run(step, act, before)
            save_pooled(GROUPS - 1, GROUP_TILES - 2)
            save_pooled(GROUPS - 1, GROUP_TILES - 1)
            save_out2(GROUPS - 1)

        @block.vector
        def _(dve):
            def double_rows(first, last):
                nc.vector.tensor_copy(rows[:, FIELDS + first:FIELDS + last, :],
                                      rows[:, first:last, :]).then_inc(rows_doubled, 1)

            def c1_lows(group, c):
                dve.wait_ge(c1_high, chunk_count(group, c + 1))
                nc.vector.tensor_tensor(c1_l[:, c % 2, :], mid[:, :], c1_h[:, c % 2, :].bitcast(F32),
                                        ALU.subtract).then_inc(c1_low, 1)
                q = c % CHUNKS
                if q == 0 and c > 0:
                    keep_out1(group)
                    dve.wait_ge(out1_ready, at(group, 1, 1))
                nc.vector.tensor_reduce(out1[:, q * CHUNK_SAMPLES:(q + 1) * CHUNK_SAMPLES],
                                        mid[:, :].rearrange("m (b d) -> m b d", d=EMB), AX_X,
                                        ALU.add).then_inc(out1_saved, 1)

            def keep_out1(group):
                dve.wait_ge(out1_saved, chunk_count(group, CHUNKS))
                nc.vector.tensor_copy(out1_done[:, :], out1[:, :]).then_inc(out1_ready, 1)

            def sum_terms(group, t, part):
                dve.wait_ge(act_bank_done, act_count(group, t + 1, 0))
                dve.wait_ge(dve_unit_done, dve_count(group, t + 1, 0))
                if not (isinstance(group, int) and group == 0 and t < 2):
                    dve.wait_ge(pool_ready, tile_count(group, t - 1))
                cols = slice(part * MAPS // SUM_PARTS, (part + 1) * MAPS // SUM_PARTS)
                nc.vector.tensor_reduce(c2[:, t % 2, cols],
                                        terms[:, t % 2, :, cols].rearrange("p s m -> p m s"), AX_X,
                                        ALU.add).then_inc(c2_ready, 1)

            def save_out3(group):
                dve.wait_ge(cross3_ready, at(group, 1, 1))
                nc.vector.tensor_copy(out3[:, :], aux[:, 0:P]).then_inc(out3_ready, 1)

            def relu(ready, saved, dst, bias, n, group):
                dve.wait_ge(ready, at(group, 1, 1))
                for j in range(n):
                    v = nc.vector.tensor_scalar(dst[:, j, :], aux[:, j * P:(j + 1) * P], bias[:, j:j + 1], 0.0,
                                                ALU.add, ALU.max)
                v.then_inc(saved, 1)

            def save_y(group):
                dve.wait_ge(y_ready, at(group, 1, 1))
                nc.vector.tensor_scalar(y_sb[:, bass.ds(group * P, P)], aux[0:1, 0:P], 1.0, None,
                                        ALU.mult).then_inc(y_saved, 1)

            def before():
                nc.vector.memset(w0_b_raw[:, PAIR_BLOCKS - 1, :], 0.0).then_inc(w0_zeroed, 1)
                full = PAIR_BLOCKS - 1
                dve.wait_ge(w0_zeroed, 1)
                dve.wait_ge(w0_loaded, 16 * 4)
                parts = ((slice(0, BLOCK), slice(0, full)),
                         (slice(0, block_rows(full)), slice(full, PAIR_BLOCKS)))
                for r, k in parts:
                    v = nc.vector.tensor_tensor(w0_sum[r, k, :], w0_a_raw[r, k, :], w0_b_raw[r, k, :], ALU.add)
                v.then_inc(w0_ready, 1)
                dve.wait_ge(w1_loaded, 16)
                nc.vector.tensor_copy(w1_h[:, :], w1_raw).then_inc(w1_high, 1)
                dve.wait_ge(w1_high, 1)
                nc.vector.tensor_tensor(w1_l[:, :], w1_raw, w1_h[:, :].bitcast(F32),
                                        ALU.subtract).then_inc(w1_ready, 1)
                dve.wait_ge(early_rows_loaded, 16 * EARLY_ROWS)
                double_rows(0, EARLY_ROWS)
                dve.wait_ge(rows_loaded, rows_count(0))
                double_rows(EARLY_ROWS, FIELDS)
                dve.wait_ge(one_copied, 1)
                for k in range(PAIR_BLOCKS):
                    if k < PE_SPREAD:
                        dve.wait_ge(pe_spread, k + 2)
                        nc.vector.tensor_tensor(pairs[:, 0, k, :], prod[0:BLOCK, k + 1, :], pair_one[:, 0, :],
                                                ALU.mult).then_inc(first_pairs_ready, 1)
                    else:
                        dve.wait_ge(other_loaded[0][k], 16 * len(block_shifts(k)))
                        make_pairs(nc.vector, 0, k, first_pairs_ready)
                c1_lows(0, 0)

            def step(group, t):
                c, i = t // TILES, t % TILES
                for j in range(BANKS):
                    if j in DVE_BANKS:
                        if j == DVE_BANKS[0]:
                            dve.wait_ge(x_col_ready, chunk_count(group, c + 1))
                            if not (isinstance(group, int) and group == 0 and t < 2):
                                dve.wait_ge(c2_ready, tile_count(group, t - 1, SUM_PARTS))
                        dve.wait_ge(prod_ready, tile_count(group, t, BANKS) + (j + 1))
                        for f in bank_fields(j):
                            b, n = f % BANK_FIELDS, DVE_ORDER.index(f)
                            src = prod[:, (BANKS * t + j) % RING, b * MAPS:(b + 1) * MAPS]
                            x = x_col[:, c % CHUNKS, i, f:f + 1]
                            acc = terms[:, t % 2, SLOTS - 2 + n % 2, :]
                            if n < 2:
                                v = nc.vector.tensor_scalar(acc, src, x, None, ALU.mult)
                            else:
                                dve.wait_ge(dve_unit_done, dve_count(group, t, n - 1))
                                v = nc.vector.scalar_tensor_tensor(out=acc, in0=src, scalar=x, in1=acc,
                                                                   op0=ALU.mult, op1=ALU.add)
                            v.then_inc(dve_unit_done, 1)
                    if j in SUM_BANKS and not is_start(group, t):
                        sum_terms(group, t - 1, SUM_BANKS.index(j))
                    pos = BANKS * i + j
                    if not (is_last(group) and c + 1 >= CHUNKS):
                        if pos == POS_C1_LOW:
                            c1_lows(group, c + 1)
                        if (c + 1) % CHUNKS == DVE_CHUNK and pos in DVE_PAIRS:
                            wait_spread(dve, group, c + 1, DVE_PAIRS[pos])
                            make_pairs(nc.vector, c + 1, DVE_PAIRS[pos], dve_pairs_ready)
                    if c % CHUNKS == 2 and pos == POS_ROWS and not is_last(group):
                        dve.wait_ge(rows_loaded, rows_count(group + 1))
                        double_rows(0, FIELDS)
                    n = BANKS * t + j
                    if n == POS_OUT3:
                        save_out3(group)
                    if n == POS_RELU1:
                        relu(h1_ready, h1_saved, h1, bt1_sb, MLP1 // P, group)
                    if n == POS_RELU2:
                        relu(h2_ready, h2_saved, h2, bt2_sb, MLP2 // P, group)
                    if n == POS_Y:
                        save_y(group)

            run(step, dve, before)
            last = GROUPS - 1
            for part in range(SUM_PARTS):
                sum_terms(last, GROUP_TILES - 1, part)
            keep_out1(last)
            save_out3(last)
            relu(h1_ready, h1_saved, h1, bt1_sb, MLP1 // P, last)
            relu(h2_ready, h2_saved, h2, bt2_sb, MLP2 // P, last)
            save_y(last)


def kernel(**inputs):
    import concourse.bacc as bacc
    from concourse.bass_utils import run_bass_kernel_spmd

    f = np.tile(np.arange(FIELDS), SHIFTS)
    g = (f + SHIFT0 + np.repeat(np.arange(SHIFTS), FIELDS)) % FIELDS
    w0 = np.asarray(inputs["L0_rec_f0"])
    members = np.concatenate([f[:BLOCK], g[:PE_SPREAD * BLOCK]]).reshape(PE_SPREAD + 1, BLOCK)
    select = (members == np.arange(FIELDS)[:, None, None]).astype(np.float32)
    arrays = {
        "ids": np.asarray(inputs["ids"]),
        "dense_t": np.asarray(inputs["dense_ctx"]).T,
        "w0_a": w0[f * FIELDS + g],
        "w0_b": w0[(g * FIELDS + f)[:CROSS]],
        "select": select,
        "w1": inputs["L0_rec_f1"],
        "w2": inputs["L0_rec_f2"],
        "wt1": inputs["W_top1"],
        "bt1": np.asarray(inputs["b_top1"]).reshape(MLP1 // P, P).T,
        "wt2": inputs["W_top2"],
        "bt2": np.asarray(inputs["b_top2"]).reshape(MLP2 // P, P).T,
        "wt3": np.asarray(inputs["W_top3"]).reshape(MLP2 // P, P).T,
    }
    for n in range(FIELDS):
        arrays[f"tbl_{n}"] = inputs[f"tbl_{n}"]
    arrays = {n: np.ascontiguousarray(a) for n, a in arrays.items()}

    nc = bacc.Bacc("TRN2", target_bir_lowering=False, num_devices=1)
    ap = {n: nc.dram_tensor(n, a.shape, mybir.dt.from_np(a.dtype), kind="ExternalInput").ap()
          for n, a in arrays.items()}
    out = nc.dram_tensor("y", (1, BATCH), F32, kind="ExternalOutput").ap()
    cin_program(nc, ap["ids"], [ap[f"tbl_{n}"] for n in range(FIELDS)], ap["dense_t"], ap["w0_a"], ap["w0_b"],
                ap["w1"], ap["w2"], ap["wt1"], ap["bt1"], ap["wt2"], ap["bt2"], ap["wt3"],
                ap["select"], out)
    result = run_bass_kernel_spmd(nc, [arrays], core_ids=[0])
    return result.results[0]["y"].reshape(BATCH, 1)
```
